# Optimizing a Trainium2 kernel written in Bass

```python
import numpy as np
import jax
import jax.numpy as jnp

def _softmax(x, axis=-1):
    return jax.nn.softmax(x, axis=axis)
def _gelu(x):
    return jax.nn.gelu(x, approximate=True)
def _silu(x):
    return jax.nn.silu(x)
def _sigmoid(x):
    return jax.nn.sigmoid(x)
def _layernorm(x, axis=-1, eps=1e-5):
    m = jnp.mean(x, axis=axis, keepdims=True)
    v = jnp.var(x, axis=axis, keepdims=True)
    return (x - m) / jnp.sqrt(v + eps)
def _scatter_add(tgt, idx, src, axis=0):
    return tgt.at[idx].add(src)
def _segment_sum(src, seg, n):
    return jax.ops.segment_sum(src, seg, n)

kernel_name = 'mk_conv_seq_d2_conv_nchw256_4d3ffd'

def setup_inputs(seed: int = 0):
    np.random.seed(seed)
    _w = jnp.asarray
    def _rec_inputs():
        import jax
        import jax.numpy as jnp
        _gk = jax.random.key(seed)
        x = -0.0005207 + 1.001 * jax.random.normal(jax.random.fold_in(_gk, 1), (8, 256, 32, 32), jnp.float32)
        return x
    x = _rec_inputs()
    def _L0_conv_setup():
        import jax, jax.numpy as jnp
        import numpy as np
        DIM = 256
        DT_RANK = 32
        D_STATE = 16
        DEPTH = 12
        B, H, W = (8, 32, 32)
        LN_EPS = 1e-05

        def _ssm(x, dbc_w, dtp_w, dtp_b, A_log, Dp):
            A = -jnp.exp(A_log)
            dbc = jnp.einsum('bld,ed->ble', x, dbc_w)
            delta, Bm, Cm = jnp.split(dbc, [DT_RANK, DT_RANK + D_STATE], axis=-1)
            delta = jax.nn.softplus(jnp.einsum('blr,dr->bld', delta, dtp_w) + dtp_b)
            dA = jnp.exp(delta[..., None] * A)
            dBu = delta[..., None] * Bm[:, :, None, :] * x[..., None]

            def step(h, inputs):
                dA_t, dBu_t, C_t = inputs
                h = dA_t * h + dBu_t
                y = jnp.einsum('bdn,bn->bd', h, C_t)
                return (h, y)
            h0 = jnp.zeros((x.shape[0], x.shape[2], D_STATE), x.dtype)
            _, ys = jax.lax.scan(step, h0, (dA.transpose(1, 0, 2, 3), dBu.transpose(1, 0, 2, 3), Cm.transpose(1, 0, 2)))
            y = ys.transpose(1, 0, 2)
            return y + x * Dp

        def _block(x, p):
            ln_g, ln_b, pw, pb, cfw, cfb, cbw, cbb, dbcw, dtpw, dtpb, alog, dp = p
            skip = x
            mu = x.mean(-1, keepdims=True)
            var = ((x - mu) ** 2).mean(-1, keepdims=True)
            xn = (x - mu) / jnp.sqrt(var + LN_EPS) * ln_g + ln_b
            xp = jnp.einsum('bld,ed->ble', xn, pw) + pb
            z = jax.nn.silu(xp)
            xf = jax.nn.softplus(jnp.einsum('bld,ed->ble', xp, cfw) + cfb)
            x1 = _ssm(xf, dbcw, dtpw, dtpb, alog, dp)
            xr = xp[:, ::-1, :]
            xb = jax.nn.softplus(jnp.einsum('bld,ed->ble', xr, cbw) + cbb)
            x2 = _ssm(xb, dbcw, dtpw, dtpb, alog, dp)[:, ::-1, :]
            return x1 * z + x2 * z + skip
        key = jax.random.key(seed)
        ks = jax.random.split(key, 8)
        d, r, n, L = (DIM, DT_RANK, D_STATE, DEPTH)

        def nrm(k, shape, scale=0.02):
            return jax.random.normal(k, shape, dtype=jnp.float32) * scale
        A_log = jnp.tile(jnp.log(jnp.arange(1, n + 1, dtype=jnp.float32))[None, None, :], (L, d, 1))
        return {'x': jax.random.normal(ks[0], (B, d, H, W), dtype=jnp.float32), 'ln_g': jnp.ones((L, d), jnp.float32), 'ln_b': jnp.zeros((L, d), jnp.float32), 'proj_w': nrm(ks[1], (L, d, d)), 'proj_b': jnp.zeros((L, d), jnp.float32), 'convf_w': nrm(ks[2], (L, d, d)), 'convf_b': jnp.zeros((L, d), jnp.float32), 'convb_w': nrm(ks[3], (L, d, d)), 'convb_b': jnp.zeros((L, d), jnp.float32), 'dbc_w': nrm(ks[4], (L, r + 2 * n, d)), 'dtp_w': nrm(ks[5], (L, d, r)), 'dtp_b': jnp.zeros((L, d), jnp.float32), 'A_log': A_log, 'D_param': jnp.ones((L, d), jnp.float32)}
    _L0_conv_all = _L0_conv_setup()
    _L0_conv_in = {k: v for k, v in _L0_conv_all.items() if k in ('ln_g', 'ln_b', 'proj_w', 'proj_b', 'convf_w', 'convf_b', 'convb_w', 'convb_b', 'dbc_w', 'dtp_w', 'dtp_b', 'A_log', 'D_param', )}
    del _L0_conv_all

    def _L1_conv_setup():
        import jax, jax.numpy as jnp
        import numpy as np
        from jax import lax
        EPS = 1e-05

        def haar_dwt(x):
            B, C, H, W = x.shape
            xr = x.reshape(B, C, H // 2, 2, W // 2, 2)
            a = xr[:, :, :, 0, :, 0]
            b = xr[:, :, :, 0, :, 1]
            c = xr[:, :, :, 1, :, 0]
            d = xr[:, :, :, 1, :, 1]
            ll = (a + b + c + d) * 0.5
            lh = (a + b - c - d) * 0.5
            hl = (a - b + c - d) * 0.5
            hh = (a - b - c + d) * 0.5
            return (ll, lh, hl, hh)

        def haar_idwt(ll, lh, hl, hh):
            B, C, h, w = ll.shape
            a = (ll + lh + hl + hh) * 0.5
            b = (ll + lh - hl - hh) * 0.5
            c = (ll - lh + hl - hh) * 0.5
            d = (ll - lh - hl + hh) * 0.5
            out = jnp.stack([jnp.stack([a, b], axis=-1), jnp.stack([c, d], axis=-1)], axis=-2)
            out = out.transpose(0, 1, 2, 4, 3, 5).reshape(B, C, 2 * h, 2 * w)
            return out

        def conv1x1(x, w, b=None):
            y = jnp.einsum('oc,bchw->bohw', w, x)
            if b is not None:
                y = y + b[None, :, None, None]
            return y

        def bn_eval(x, g, b, m, v):
            inv = g * lax.rsqrt(v + EPS)
            return x * inv[None, :, None, None] + (b - m * inv)[None, :, None, None]
        key = jax.random.key(seed)
        ks = jax.random.split(key, 12)
        B, C, H, W = (8, 256, 160, 160)
        hid = C // 16
        f32 = jnp.float32
        x = jax.random.normal(ks[0], (B, C, H, W), f32)
        fusion_w = jax.random.normal(ks[1], (C, 4 * C), f32) * (1.0 / np.sqrt(4 * C))
        fusion_b = jnp.zeros((C,), f32)
        bn1_g = jnp.ones((C,), f32)
        bn1_b = jnp.zeros((C,), f32)
        bn1_m = jax.random.normal(ks[2], (C,), f32) * 0.1
        bn1_v = jax.random.uniform(ks[3], (C,), f32, 0.5, 1.5)
        sa_w = jax.random.normal(ks[4], (1, 2, 7, 7), f32) * (1.0 / np.sqrt(2 * 49))
        ca_w1 = jax.random.normal(ks[5], (hid, C), f32) * (1.0 / np.sqrt(C))
        ca_w2 = jax.random.normal(ks[6], (C, hid), f32) * (1.0 / np.sqrt(hid))
        proj_w = jax.random.normal(ks[7], (4 * C, C), f32) * (1.0 / np.sqrt(C))
        proj_b = jnp.zeros((4 * C,), f32)
        bn2_g = jnp.ones((4 * C,), f32)
        bn2_b = jnp.zeros((4 * C,), f32)
        bn2_m = jax.random.normal(ks[8], (4 * C,), f32) * 0.1
        bn2_v = jax.random.uniform(ks[9], (4 * C,), f32, 0.5, 1.5)
        return dict(x=x, fusion_w=fusion_w, fusion_b=fusion_b, bn1_g=bn1_g, bn1_b=bn1_b, bn1_m=bn1_m, bn1_v=bn1_v, sa_w=sa_w, ca_w1=ca_w1, ca_w2=ca_w2, proj_w=proj_w, proj_b=proj_b, bn2_g=bn2_g, bn2_b=bn2_b, bn2_m=bn2_m, bn2_v=bn2_v)
    _L1_conv_all = _L1_conv_setup()
    _L1_conv_in = {k: v for k, v in _L1_conv_all.items() if k in ('fusion_w', 'fusion_b', 'bn1_g', 'bn1_b', 'bn1_m', 'bn1_v', 'sa_w', 'ca_w1', 'ca_w2', 'proj_w', 'proj_b', 'bn2_g', 'bn2_b', 'bn2_m', 'bn2_v', )}
    del _L1_conv_all

    return {
        "x": x,
        "L0_conv_ln_g": _L0_conv_in["ln_g"],
        "L0_conv_ln_b": _L0_conv_in["ln_b"],
        "L0_conv_proj_w": _L0_conv_in["proj_w"],
        "L0_conv_proj_b": _L0_conv_in["proj_b"],
        "L0_conv_convf_w": _L0_conv_in["convf_w"],
        "L0_conv_convf_b": _L0_conv_in["convf_b"],
        "L0_conv_convb_w": _L0_conv_in["convb_w"],
        "L0_conv_convb_b": _L0_conv_in["convb_b"],
        "L0_conv_dbc_w": _L0_conv_in["dbc_w"],
        "L0_conv_dtp_w": _L0_conv_in["dtp_w"],
        "L0_conv_dtp_b": _L0_conv_in["dtp_b"],
        "L0_conv_A_log": _L0_conv_in["A_log"],
        "L0_conv_D_param": _L0_conv_in["D_param"],
        "L1_conv_fusion_w": _L1_conv_in["fusion_w"],
        "L1_conv_fusion_b": _L1_conv_in["fusion_b"],
        "L1_conv_bn1_g": _L1_conv_in["bn1_g"],
        "L1_conv_bn1_b": _L1_conv_in["bn1_b"],
        "L1_conv_bn1_m": _L1_conv_in["bn1_m"],
        "L1_conv_bn1_v": _L1_conv_in["bn1_v"],
        "L1_conv_sa_w": _L1_conv_in["sa_w"],
        "L1_conv_ca_w1": _L1_conv_in["ca_w1"],
        "L1_conv_ca_w2": _L1_conv_in["ca_w2"],
        "L1_conv_proj_w": _L1_conv_in["proj_w"],
        "L1_conv_proj_b": _L1_conv_in["proj_b"],
        "L1_conv_bn2_g": _L1_conv_in["bn2_g"],
        "L1_conv_bn2_b": _L1_conv_in["bn2_b"],
        "L1_conv_bn2_m": _L1_conv_in["bn2_m"],
        "L1_conv_bn2_v": _L1_conv_in["bn2_v"],
    }

def reference(x, L0_conv_ln_g, L0_conv_ln_b, L0_conv_proj_w, L0_conv_proj_b, L0_conv_convf_w, L0_conv_convf_b, L0_conv_convb_w, L0_conv_convb_b, L0_conv_dbc_w, L0_conv_dtp_w, L0_conv_dtp_b, L0_conv_A_log, L0_conv_D_param, L1_conv_fusion_w, L1_conv_fusion_b, L1_conv_bn1_g, L1_conv_bn1_b, L1_conv_bn1_m, L1_conv_bn1_v, L1_conv_sa_w, L1_conv_ca_w1, L1_conv_ca_w2, L1_conv_proj_w, L1_conv_proj_b, L1_conv_bn2_g, L1_conv_bn2_b, L1_conv_bn2_m, L1_conv_bn2_v):
    import jax
    import jax.numpy as jnp
    def _L0_conv_ref(x, ln_g, ln_b, proj_w, proj_b, convf_w, convf_b, convb_w, convb_b, dbc_w, dtp_w, dtp_b, A_log, D_param):
        import jax, jax.numpy as jnp
        import numpy as np
        DIM = 256
        DT_RANK = 32
        D_STATE = 16
        DEPTH = 12
        B, H, W = (8, 32, 32)
        LN_EPS = 1e-05

        def _ssm(x, dbc_w, dtp_w, dtp_b, A_log, Dp):
            A = -jnp.exp(A_log)
            dbc = jnp.einsum('bld,ed->ble', x, dbc_w)
            delta, Bm, Cm = jnp.split(dbc, [DT_RANK, DT_RANK + D_STATE], axis=-1)
            delta = jax.nn.softplus(jnp.einsum('blr,dr->bld', delta, dtp_w) + dtp_b)
            dA = jnp.exp(delta[..., None] * A)
            dBu = delta[..., None] * Bm[:, :, None, :] * x[..., None]

            def step(h, inputs):
                dA_t, dBu_t, C_t = inputs
                h = dA_t * h + dBu_t
                y = jnp.einsum('bdn,bn->bd', h, C_t)
                return (h, y)
            h0 = jnp.zeros((x.shape[0], x.shape[2], D_STATE), x.dtype)
            _, ys = jax.lax.scan(step, h0, (dA.transpose(1, 0, 2, 3), dBu.transpose(1, 0, 2, 3), Cm.transpose(1, 0, 2)))
            y = ys.transpose(1, 0, 2)
            return y + x * Dp

        def _block(x, p):
            ln_g, ln_b, pw, pb, cfw, cfb, cbw, cbb, dbcw, dtpw, dtpb, alog, dp = p
            skip = x
            mu = x.mean(-1, keepdims=True)
            var = ((x - mu) ** 2).mean(-1, keepdims=True)
            xn = (x - mu) / jnp.sqrt(var + LN_EPS) * ln_g + ln_b
            xp = jnp.einsum('bld,ed->ble', xn, pw) + pb
            z = jax.nn.silu(xp)
            xf = jax.nn.softplus(jnp.einsum('bld,ed->ble', xp, cfw) + cfb)
            x1 = _ssm(xf, dbcw, dtpw, dtpb, alog, dp)
            xr = xp[:, ::-1, :]
            xb = jax.nn.softplus(jnp.einsum('bld,ed->ble', xr, cbw) + cbb)
            x2 = _ssm(xb, dbcw, dtpw, dtpb, alog, dp)[:, ::-1, :]
            return x1 * z + x2 * z + skip
        b, c, h, w = x.shape
        seq = x.reshape(b, c, h * w).transpose(0, 2, 1)
        params = (ln_g, ln_b, proj_w, proj_b, convf_w, convf_b, convb_w, convb_b, dbc_w, dtp_w, dtp_b, A_log, D_param)

        def layer_step(s, p):
            return (_block(s, p), None)
        seq, _ = jax.lax.scan(layer_step, seq, params)
        return seq.transpose(0, 2, 1).reshape(b, c, h, w)

    def _L1_conv_ref(x, fusion_w, fusion_b, bn1_g, bn1_b, bn1_m, bn1_v, sa_w, ca_w1, ca_w2, proj_w, proj_b, bn2_g, bn2_b, bn2_m, bn2_v):
        import jax, jax.numpy as jnp
        import numpy as np
        from jax import lax
        EPS = 1e-05

        def haar_dwt(x):
            B, C, H, W = x.shape
            xr = x.reshape(B, C, H // 2, 2, W // 2, 2)
            a = xr[:, :, :, 0, :, 0]
            b = xr[:, :, :, 0, :, 1]
            c = xr[:, :, :, 1, :, 0]
            d = xr[:, :, :, 1, :, 1]
            ll = (a + b + c + d) * 0.5
            lh = (a + b - c - d) * 0.5
            hl = (a - b + c - d) * 0.5
            hh = (a - b - c + d) * 0.5
            return (ll, lh, hl, hh)

        def haar_idwt(ll, lh, hl, hh):
            B, C, h, w = ll.shape
            a = (ll + lh + hl + hh) * 0.5
            b = (ll + lh - hl - hh) * 0.5
            c = (ll - lh + hl - hh) * 0.5
            d = (ll - lh - hl + hh) * 0.5
            out = jnp.stack([jnp.stack([a, b], axis=-1), jnp.stack([c, d], axis=-1)], axis=-2)
            out = out.transpose(0, 1, 2, 4, 3, 5).reshape(B, C, 2 * h, 2 * w)
            return out

        def conv1x1(x, w, b=None):
            y = jnp.einsum('oc,bchw->bohw', w, x)
            if b is not None:
                y = y + b[None, :, None, None]
            return y

        def bn_eval(x, g, b, m, v):
            inv = g * lax.rsqrt(v + EPS)
            return x * inv[None, :, None, None] + (b - m * inv)[None, :, None, None]
        identity = x
        ll, lh, hl, hh = haar_dwt(x)
        wav = jnp.concatenate([ll, lh, hl, hh], axis=1)
        fused = jax.nn.relu(bn_eval(conv1x1(wav, fusion_w, fusion_b), bn1_g, bn1_b, bn1_m, bn1_v))
        avg_sp = jnp.mean(fused, axis=1, keepdims=True)
        max_sp = jnp.max(fused, axis=1, keepdims=True)
        sp_in = jnp.concatenate([avg_sp, max_sp], axis=1)
        sp_map = lax.conv_general_dilated(sp_in, sa_w, (1, 1), ((3, 3), (3, 3)), dimension_numbers=('NCHW', 'OIHW', 'NCHW'))
        spatial_out = jax.nn.sigmoid(sp_map) * fused
        avg_ch = jnp.mean(spatial_out, axis=(2, 3), keepdims=True)
        max_ch = jnp.max(spatial_out, axis=(2, 3), keepdims=True)

        def mlp(p):
            return conv1x1(jax.nn.relu(conv1x1(p, ca_w1)), ca_w2)
        ch_map = jax.nn.sigmoid(mlp(avg_ch) + mlp(max_ch))
        channel_out = ch_map * spatial_out
        projected = jax.nn.relu(bn_eval(conv1x1(channel_out, proj_w, proj_b), bn2_g, bn2_b, bn2_m, bn2_v))
        C = projected.shape[1] // 4
        ll_o = projected[:, :C]
        lh_o = projected[:, C:2 * C]
        hl_o = projected[:, 2 * C:3 * C]
        hh_o = projected[:, 3 * C:]
        reconstructed = haar_idwt(ll_o, lh_o, hl_o, hh_o)
        return reconstructed + identity

    def _gn(v, G=32, eps=1e-5):
        B_, C_, H_, W_ = v.shape
        g = v.reshape(B_, G, C_ // G, H_, W_)
        m = jnp.mean(g, axis=(2, 3, 4), keepdims=True)
        s = jnp.var(g, axis=(2, 3, 4), keepdims=True)
        return ((g - m) / jnp.sqrt(s + eps)).reshape(v.shape)

    def _ln_c(v, eps=1e-6):
        m = jnp.mean(v, axis=1, keepdims=True)
        s = jnp.var(v, axis=1, keepdims=True)
        return (v - m) / jnp.sqrt(s + eps)

    def _ln_t(v, eps=1e-5):
        m = jnp.mean(v, axis=-1, keepdims=True)
        s = jnp.var(v, axis=-1, keepdims=True)
        return (v - m) / jnp.sqrt(s + eps)

    def _to_tokens(v):
        B_, C_, H_, W_ = v.shape
        return v.reshape(B_, C_, H_ * W_).transpose(0, 2, 1)
    def _from_tokens(t, like):
        B_, C_, H_, W_ = like.shape
        return t.transpose(0, 2, 1).reshape(B_, C_, H_, W_)

    x = _L0_conv_ref(x, L0_conv_ln_g, L0_conv_ln_b, L0_conv_proj_w, L0_conv_proj_b, L0_conv_convf_w, L0_conv_convf_b, L0_conv_convb_w, L0_conv_convb_b, L0_conv_dbc_w, L0_conv_dtp_w, L0_conv_dtp_b, L0_conv_A_log, L0_conv_D_param)
    x = _L1_conv_ref(x, L1_conv_fusion_w, L1_conv_fusion_b, L1_conv_bn1_g, L1_conv_bn1_b, L1_conv_bn1_m, L1_conv_bn1_v, L1_conv_sa_w, L1_conv_ca_w1, L1_conv_ca_w2, L1_conv_proj_w, L1_conv_proj_b, L1_conv_bn2_g, L1_conv_bn2_b, L1_conv_bn2_m, L1_conv_bn2_v)
    return x


_drawn_inputs = setup_inputs


def setup_inputs(seed=0):
    import zlib

    import numpy as np

    out = dict(_drawn_inputs(seed))
    spreads = {'L0_conv_ln_g': (1.0, 0.2),
     'L0_conv_ln_b': (0.0, 0.1),
     'L0_conv_proj_b': (0.0, 0.1),
     'L0_conv_convf_b': (0.0, 0.323),
     'L0_conv_convb_b': (0.0, 0.323),
     'L0_conv_dtp_b': (0.0, 0.8),
     'L0_conv_D_param': (1.0, 0.2),
     'L1_conv_fusion_b': (0.0, 0.39),
     'L1_conv_bn1_g': (1.0, 0.2),
     'L1_conv_bn1_b': (0.0, 0.493),
     'L1_conv_proj_b': (0.0, 0.1),
     'L1_conv_bn2_g': (1.0, 0.2),
     'L1_conv_bn2_b': (0.0, 0.1)}
    factors = {'L0_conv_dtp_w': 26.739, 'L1_conv_bn1_m': 2.697}
    for name, (base, spread) in spreads.items():
        noise = np.random.default_rng([zlib.crc32(name.encode()), seed]).standard_normal(out[name].shape)
        drawn = base * np.exp(spread * noise) if base else spread * noise
        out[name] = jnp.asarray(drawn.astype(out[name].dtype))
    for name, factor in factors.items():
        out[name] = (out[name] * factor).astype(out[name].dtype)
    return out
```

```python
from contextlib import ExitStack

import concourse.bass as bass
from concourse import mybir

F32 = mybir.dt.float32
BF16 = mybir.dt.bfloat16
ALU = mybir.AluOpType
ACT = mybir.ActivationFunctionType

P = 128
LAYERS = 12
B = 8
C = 256
H2 = C // P
L = 1024
T = 512
N = 16
R = 32
ITEMS = LAYERS * B
SEGS = 4
CHUNK = [0, 1, 1, 0]
STEPS = SEGS * N
SOFTPLUSES = 2 * SEGS

W_PROJ = 0
W_CONV = [W_PROJ + H2 * C, W_PROJ + 2 * H2 * C]
W_DBC = W_CONV[1] + H2 * C
W_DT = W_DBC + H2 * P
W_G = W_DT + C
W_B = W_G + H2
W_PB = W_B + H2
W_CB = [W_PB + H2, W_PB + 2 * H2]
W_DTB = W_CB[1] + H2
W_D = W_DTB + H2
W_A = W_D + H2
W_COLS = W_A + H2 * N

USES = [("bias", 11), ("mean0", 12), ("var0", 15), ("proj00", 19), ("proj01", 20),
        ("conv00", 21), ("conv01", 22), ("mean1", 24), ("dbc0", 27), ("var1", 29),
        ("dt00", 30), ("dt01", 31), ("proj10", 33), ("proj11", 34),
        ("conv10", 35), ("conv11", 36), ("dbc1", 41), ("dt10", 43), ("dt11", 44),
        ("conv20", 45), ("conv21", 46), ("dbc2", 51), ("dt20", 53), ("dt21", 54),
        ("conv30", 55), ("conv31", 56), ("dbc3", 61), ("dt30", 63), ("dt31", 64)]
NU = len(USES)
USE = {name: k for k, (name, _) in enumerate(USES)}
AT = dict(USES)
DENSE_END = 75


def scan_layers(nc, x_in, w_all, const_in, x_dram):
    with ExitStack() as ctx:
        def sb(name, shape, dt=F32):
            return ctx.enter_context(nc.sbuf_tensor(name, shape, dt))

        def ps(name, shape):
            return ctx.enter_context(nc.psum_tensor(name, shape, F32))

        def sem(name):
            return ctx.enter_context(nc.semaphore(name))

        const = sb("const", [P, P + 2 + 2 * N])
        ident = const[:, 0:P]
        neg_mask = [const[0:96, P:P + 1], const[0:96, P + 1:P + 2]]
        ones = sb("ones", [P, P])
        eps = sb("eps", [P, 1])
        sel = sb("sel", [96, 2 * N], BF16)
        w = [sb(f"w{p}", [P, W_COLS]) for p in range(2)]
        x = [sb(f"x{p}", [P, 2, H2, T]) for p in range(2)]
        z = [sb(f"z{p}", [P, 2, H2, T]) for p in range(2)]
        xs = [sb(f"xs{p}", [P, 2, H2, T]) for p in range(2)]
        negA = [sb(f"negA{p}", [P, H2, N]) for p in range(2)]
        expA = sb("expA", [P, H2 * N])
        diagD = [sb(f"diagD{p}", [P, H2, P]) for p in range(2)]
        gW = sb("gW", [P, H2, C])
        pbias = sb("pbias", [P, H2])
        delta = sb("delta", [P, SEGS, H2, T])
        u = sb("u", [P, SEGS, H2, T])
        bc = sb("bc", [96, SEGS, T], BF16)
        xc = sb("xc", [P, H2, T])
        sq = sb("sq", [P, H2, T])
        lnv = sb("lnv", [P, T])
        rstd = sb("rstd", [P, T])
        xp = sb("xp", [P, 2, H2, T])
        a_conv = sb("a_conv", [P, H2, T])
        a_dt = sb("a_dt", [P, H2, T])
        xb = sb("xb", [P, 2, H2, T])
        bc_hi = sb("bc_hi", [96, T], BF16)
        bc_mid = sb("bc_mid", [96, T], BF16)
        bc_rest = sb("bc_rest", [96, T])
        dt_low = sb("dt_low", [P, T])
        bB = sb("bB", [P, 4, T])
        du = sb("du", [P, 4, H2, T])
        hh = sb("hh", [P, 4, H2, T])
        state = sb("state", [P, N, H2])
        prod = sb("prod", [P, 2, H2, T])
        y_save = sb("y_save", [P, H2, T])
        yz = sb("yz", [P, H2, T])

        psA = ps("psA", [P, H2, T])
        psC = ps("psC", [P, 2, T])
        psY = ps("psY", [P, H2, T])
        psB = ps("psB", [P, T])
        psD = ps("psD", [P, T])

        const_loaded = sem("const_loaded")
        ones_set = sem("ones_set")
        sel_set = sem("sel_set")
        w_loaded = [sem(f"w_loaded{p}") for p in range(2)]
        x_loaded = [sem(f"x_loaded{p}") for p in range(2)]
        x_stored = sem("x_stored")
        psd_ready = sem("psd_ready")
        psd_free = sem("psd_free")
        sq_done = sem("sq_done")
        rstd_done = sem("rstd_done")
        xn_done = sem("xn_done")
        abs_done = sem("abs_done")
        exp_done = sem("exp_done")
        sp_ready = sem("sp_ready")
        sp_done = sem("sp_done")
        hi_done = sem("hi_done")
        mid_done = sem("mid_done")
        bc_done = sem("bc_done")
        u_done = sem("u_done")
        xs_done = sem("xs_done")
        z_done = sem("z_done")
        expA_done = sem("expA_done")
        prep_done = sem("prep_done")
        gw_done = sem("gw_done")
        b_ready = sem("b_ready")
        b_copied = sem("b_copied")
        c_ready = sem("c_ready")
        du_done = sem("du_done")
        dA_ready = sem("dA_ready")
        scan_done = sem("scan_done")
        prod_done = sem("prod_done")
        sum_done = sem("sum_done")
        state_saved = sem("state_saved")
        y_saved = sem("y_saved")
        yz_done = sem("yz_done")
        x_new = sem("x_new")

        def wait(eng, semaphore, value):
            if not isinstance(value, int) or value > 0:
                eng.wait_ge(semaphore, value)

        def run(eng, step, dense, tail):
            for t in range(STEPS):
                dense(0, 0, t)

            def pair(i0, last=False):
                for par in range(2):
                    i = i0 + par
                    for s in range(STEPS):
                        step(i, par, s)
                        if STEPS + s < DENSE_END:
                            dense(i, par, STEPS + s)
                        if not (last and par == 1):
                            dense(i + 1, 1 - par, s)

            pair(0)
            with eng.Fori(2, ITEMS - 2, 2) as i:
                pair(i)
            pair(ITEMS - 2, last=True)
            tail()

        def loads(j, par, each):
            return (j - par) * (each // 2) + each

        def forward(ap):
            return ap

        def backward(ap):
            return ap[:, ::-1]

        def segment(s):
            q, n = divmod(s, N)
            return q, n

        block = ctx.enter_context(nc.Block())

        @block.sync
        def _(sp):
            def load_w(layer, p):
                sp.dma_start(w[p][:, :], w_all[layer]).then_inc(w_loaded[p], 16)

            def item(i, layer, b):
                if not (isinstance(i, int) and i == ITEMS - 1):
                    nb, nl = (b + 1) % B, layer + (b + 1) // B
                    p = (b + 1) % 2
                    wait(sp, psd_free, i * NU)
                    load_w(nl, p)
                    sp.wait_ge(x_stored, 16 * 2 * B + i * 32)
                    for h in range(H2):
                        sp.dma_start(x[p][:, :, h, :], x_dram[nb, h]).then_inc(x_loaded[p], 16)
                for k, c in enumerate((1, 0)):
                    sp.wait_ge(x_new, 2 * i + k + 1)
                    sp.dma_start(x_dram[b, :, :, c, :].rearrange("h p t -> p h t"),
                                 x[b % 2][:, c, :, :]).then_inc(x_stored, 16)

            sp.dma_start(const[:, :], const_in).then_inc(const_loaded, 16)
            load_w(0, 0)
            for h in range(H2):
                sp.dma_start(x[0][:, :, h, :], x_in[0, h]).then_inc(x_loaded[0], 16)
            for b in range(B):
                for h in range(H2):
                    sp.dma_start(x_dram[b, h], x_in[b, h]).then_inc(x_stored, 16)
            for b in range(B):
                item(b, 0, b)
            with sp.Fori(1, LAYERS - 1) as layer:
                for b in range(B):
                    item(layer * B + b, layer, b)
            for b in range(B):
                item((LAYERS - 1) * B + b, LAYERS - 1, b)
            sp.wait_ge(x_stored, 16 * 2 * B + ITEMS * 32)

        @block.tensor
        def _(pe):
            def spread(out, row, q):
                return pe.matmul(out, sel[:, row:row + 1].broadcast_to([96, P]), bc[:, q, :],
                                 start=True, stop=True)

            def spread_b(i, s):
                if s >= STEPS:
                    i, s = i + 1, s - STEPS
                q, n = segment(s)
                g = i * STEPS + s
                if n == 0:
                    wait(pe, bc_done, i * SEGS + q + 1)
                wait(pe, b_copied, g)
                spread(psB[:, :], n, q).then_inc(b_ready, 1)

            def sum_states(i, par, s):
                q, n = segment(s)
                g = i * STEPS + s
                first = s in (0, N, 3 * N)
                if s == 0:
                    wait(pe, yz_done, 2 * i)
                if s == N:
                    wait(pe, y_saved, i + 1)
                if s == 3 * N:
                    wait(pe, yz_done, 2 * i + 1)
                if s in (N, 3 * N):
                    c = 1 if s == N else 0
                    wait(pe, xs_done, 2 * i + 2 - c)
                    for h in range(H2):
                        pe.matmul(psY[:, h, :], diagD[par][:, h, :], xs[par][:, c, h, :],
                                  start=True, stop=False)
                if s == 3 * N:
                    for h in range(H2):
                        pe.matmul(psY[:, h, :], ident, y_save[:, h, :], start=False, stop=False)
                last = s in (N - 1, 3 * N - 1, STEPS - 1)
                wait(pe, prod_done, g + 1)
                for h in range(H2):
                    mm = pe.matmul(psY[:, h, :], ident, prod[:, s % 2, h, :],
                                   start=(s == 0), stop=last)
                mm.then_inc(sum_done, 1)

            def step(i, par, s):
                q, n = segment(s)
                g = i * STEPS + s
                if not (isinstance(i, int) and i == ITEMS - 1 and s + 3 >= STEPS):
                    spread_b(i, s + 3)
                wait(pe, prod_done, g - 1)
                spread(psC[:, s % 2, :], N + n, q).then_inc(c_ready, 1)
                if s >= 2:
                    sum_states(i, par, s - 2)
                elif not (isinstance(i, int) and i == 0):
                    sum_states(i - 1, 1 - par, STEPS + s - 2)

            def dense(j, par, t):
                for name, at in USES:
                    if at != t:
                        continue
                    k = USE[name]
                    wait(pe, psd_free, j * NU + k)
                    if name == "bias":
                        wait(pe, w_loaded[par], loads(j, par, 16))
                        for e in range(H2):
                            for h in range(H2):
                                mm = pe.matmul(psD[:, e:e + 1],
                                               w[par][:, W_PROJ + h * C + e * P:W_PROJ + h * C + (e + 1) * P],
                                               w[par][:, W_B + h:W_B + h + 1],
                                               start=(h == 0), stop=(h == H2 - 1))
                    elif name.startswith("mean"):
                        c = int(name[-1])
                        wait(pe, x_loaded[par], loads(j, par, 32))
                        for h in range(H2):
                            mm = pe.matmul(psD[:, :], ones[:, :], x[par][:, c, h, :],
                                           start=(h == 0), stop=(h == H2 - 1))
                    elif name.startswith("var"):
                        c = int(name[-1])
                        wait(pe, sq_done, 2 * j + c + 1)
                        for h in range(H2):
                            mm = pe.matmul(psD[:, :], ones[:, :], sq[:, h, :],
                                           start=(h == 0), stop=(h == H2 - 1))
                    elif name.startswith("proj"):
                        c, e = int(name[-2]), int(name[-1])
                        wait(pe, gw_done, j + 1)
                        wait(pe, xn_done, 2 * j + c + 1)
                        for h in range(H2):
                            mm = pe.matmul(psD[:, :], gW[:, h, e * P:(e + 1) * P], xc[:, h, :],
                                           start=(h == 0), stop=(h == H2 - 1))
                    elif name.startswith("conv"):
                        q, e = int(name[-2]), int(name[-1])
                        c, direction = CHUNK[q], q // 2
                        for h in range(H2):
                            at_w = W_CONV[direction] + h * C + e * P
                            mm = pe.matmul(psD[:, :], w[par][:, at_w:at_w + P], xp[:, c, h, :],
                                           start=(h == 0), stop=(h == H2 - 1))
                    elif name.startswith("dbc"):
                        q = int(name[-1])
                        wait(pe, sp_done, SOFTPLUSES * j + 2 * q + 1)
                        for h in range(H2):
                            src = xs[par][:, q, h, :] if q < 2 else xb[:, q - 2, h, :]
                            at_w = W_DBC + h * P
                            mm = pe.matmul(psD[:, :], w[par][:, at_w:at_w + P], src,
                                           start=(h == 0), stop=(h == H2 - 1))
                    else:
                        q, e = int(name[-2]), int(name[-1])
                        wait(pe, hi_done, SEGS * j + q + 1)
                        mm = pe.matmul(psD[:, :], w[par][96:P, W_DT + e * P:W_DT + (e + 1) * P],
                                       dt_low[96:P, :], start=True, stop=True)
                    mm.then_inc(psd_ready, 1)

            def tail():
                sum_states(ITEMS - 1, 1, STEPS - 2)
                sum_states(ITEMS - 1, 1, STEPS - 1)

            pe.wait_ge(const_loaded, 16)
            pe.wait_ge(ones_set, 2)
            pe.wait_ge(sel_set, 1)
            started = [False]

            def first_step(i, par, s):
                if not started[0]:
                    started[0] = True
                    for s0 in range(3):
                        spread_b(0, s0)
                step(i, par, s)

            run(pe, first_step, dense, tail)

        @block.scalar
        def _(act):
            def copy_b(i, s):
                g = i * STEPS + s
                wait(act, b_ready, g + 1)
                wait(act, du_done, g - 3)
                nc.scalar.activation(bB[:, s % 4, :], psB[:, :], ACT.Copy).then_inc(b_copied, 1)

            def save_state(i, s):
                q, n = segment(s)
                g = i * STEPS + s
                end = T - 1 if q == 0 else 0
                wait(act, scan_done, 2 * g + 2)
                nc.scalar.activation(state[:, n, :], hh[:, s % 4, :, end], ACT.Copy).then_inc(state_saved, 1)

            def step(i, par, s):
                q, n = segment(s)
                g = i * STEPS + s
                if n == 0:
                    wait(act, sp_done, SOFTPLUSES * i + 2 * q + 2)
                    wait(act, prep_done, i + 1)
                for h in range(H2):
                    wait(act, scan_done, 2 * g - 1 + h)
                    nc.scalar.activation(psA[:, h, :], delta[:, q, h, :], ACT.Exp,
                                         scale=negA[par][:, h, n:n + 1]).then_inc(dA_ready, 1)
                if not (isinstance(i, int) and i == ITEMS - 1 and s + 2 >= STEPS):
                    copy_b(i, s + 2)
                if 2 <= s < N + 2 or 2 * N + 2 <= s < 3 * N + 2:
                    save_state(i, s - 2)
                if s == N + 2:
                    wait(act, sum_done, i * STEPS + N)
                    nc.scalar.activation(y_save[:, :, :], psY[:, :, :], ACT.Copy).then_inc(y_saved, 1)

            def read_softplus(j, par, name):
                q, e = int(name[-2]), int(name[-1])
                if name.startswith("conv"):
                    bias = w[par][:, W_CB[q // 2] + e:W_CB[q // 2] + e + 1]
                    positive = xs[par][:, q, e, :] if q < 2 else xb[:, q - 2, e, :]
                    size = a_conv[:, e, :]
                    wait(act, sp_done, SOFTPLUSES * j + 2 * q - 1)
                    if q < 2:
                        wait(act, sum_done, (j - 1) * STEPS)
                    else:
                        wait(act, u_done, SEGS * (j - 1) + q + 1)
                        wait(act, xs_done, 2 * (j - 1) + q - 1)
                else:
                    bias = w[par][:, W_DTB + e:W_DTB + e + 1]
                    positive = delta[:, q, e, :]
                    size = a_dt[:, e, :]
                    wait(act, sp_done, SOFTPLUSES * j + 2 * q)
                    wait(act, dA_ready, 2 * ((j - 1) * STEPS + (q + 1) * N))
                    wait(act, u_done, SEGS * (j - 1) + q + 1)
                nc.scalar.activation(positive, psD[:, :], ACT.Relu, bias=bias)
                nc.scalar.activation(size, psD[:, :], ACT.Abs, bias=bias).then_inc(psd_free, 1)

            def dense(j, par, t):
                if t == 6:
                    wait(act, w_loaded[par], loads(j, par, 16))
                    wait(act, prep_done, j)
                    nc.scalar.activation(expA[:, :], w[par][:, W_A:W_A + H2 * N], ACT.Exp).then_inc(expA_done, 1)
                if t == 7:
                    wait(act, sum_done, (j - 1) * STEPS)
                    for h in range(H2):
                        nc.scalar.activation(diagD[par][:, h, :], ident, ACT.Copy,
                                             scale=w[par][:, W_D + h:W_D + h + 1])
                    wait(act, expA_done, j + 1)
                    wait(act, dA_ready, 2 * (j - 1) * STEPS)
                    nc.scalar.activation(negA[par][:, :, :], expA[:, :], ACT.Copy, scale=-1.0).then_inc(prep_done, 1)
                if t == 8:
                    wait(act, psd_ready, (j - 1) * NU + USE["proj11"] + 1)
                    for h in range(H2):
                        a = nc.scalar.activation(gW[:, h, :], w[par][:, W_PROJ + h * C:W_PROJ + (h + 1) * C],
                                                 ACT.Copy, scale=w[par][:, W_G + h:W_G + h + 1])
                    a.then_inc(gw_done, 1)
                for name, at in USES:
                    k = USE[name]
                    ready = j * NU + k + 1
                    kind = name.rstrip("0123")
                    if kind == "bias" and t == at + 1:
                        wait(act, psd_ready, ready)
                        wait(act, psd_free, (j - 1) * NU + USE["proj11"] + 1)
                        for e in range(H2):
                            a = nc.scalar.activation(pbias[:, e:e + 1], psD[:, e:e + 1], ACT.Identity,
                                                     bias=w[par][:, W_PB + e:W_PB + e + 1])
                        a.then_inc(psd_free, 1)
                    if kind == "mean" and t == at + 3:
                        c = int(name[-1])
                        wait(act, psd_free, ready)
                        wait(act, psd_ready, j * NU + USE["var0"] + 1 if c else (j - 1) * NU + USE["var1"] + 1)
                        nc.scalar.activation(sq[:, :, :], xc[:, :, :], ACT.Square).then_inc(sq_done, 1)
                    if kind == "var" and t == at + 1:
                        c = int(name[-1])
                        wait(act, psd_ready, ready)
                        wait(act, rstd_done, 2 * j + c)
                        nc.scalar.activation(lnv[:, :], psD[:, :], ACT.Ln, bias=eps[:, :]).then_inc(psd_free, 1)
                    if kind == "var" and t == at + 2:
                        c = int(name[-1])
                        wait(act, psd_free, ready)
                        wait(act, xn_done, 2 * j + c)
                        nc.scalar.activation(rstd[:, :], lnv[:, :], ACT.Exp, scale=-0.5).then_inc(rstd_done, 1)
                    if kind == "proj" and t == at + 1:
                        c, e = int(name[-2]), int(name[-1])
                        wait(act, psd_ready, ready)
                        wait(act, psd_ready, (j - 1) * NU + USE["conv31"] + 1)
                        wait(act, z_done, j)
                        wait(act, psd_free, j * NU + USE["bias"] + 1)
                        nc.scalar.activation(xp[:, c, e, :], psD[:, :], ACT.Identity,
                                             bias=pbias[:, e:e + 1]).then_inc(psd_free, 1)
                    if kind in ("conv", "dt") and t == at + 1:
                        wait(act, psd_ready, ready)
                        read_softplus(j, par, name)
                    if kind in ("conv", "dt") and name[-1] == "1" and t in (at + 2, at + 3):
                        q = int(name[-2])
                        count = SOFTPLUSES * j + 2 * q + (kind == "dt")
                        size = a_conv if kind == "conv" else a_dt
                        if t == at + 2:
                            wait(act, psd_free, ready)
                            nc.scalar.activation(size[:, :, :], size[:, :, :], ACT.Exp,
                                                 scale=-1.0).then_inc(exp_done, 1)
                        else:
                            wait(act, exp_done, count + 1)
                            nc.scalar.activation(size[:, :, :], size[:, :, :], ACT.Ln,
                                                 bias=1.0).then_inc(sp_ready, 1)
                    if kind == "dbc" and t == at + 1:
                        q = int(name[-1])
                        wait(act, psd_ready, ready)
                        nc.scalar.activation(bc_hi[:, :], psD[0:96, :], ACT.Copy)
                        nc.scalar.activation(dt_low[96:P, :], psD[96:P, :], ACT.Copy).then_inc(hi_done, 1)
                    if kind == "dbc" and t == at + 3:
                        q = int(name[-1])
                        wait(act, psd_free, ready)
                        wait(act, bc_done, SEGS * j + q)
                        nc.scalar.activation(bc_mid[:, :], bc_rest[:, :], ACT.Copy).then_inc(mid_done, 1)
                if t == 48:
                    nc.scalar.preload_act_table_set("silu_and_others")
                    wait(act, psd_free, j * NU + USE["proj11"] + 1)
                    wait(act, yz_done, 2 * (j - 1))
                    nc.scalar.activation(z[par][:, :, :, :], xp[:, :, :, :], ACT.Silu).then_inc(z_done, 1)
                    nc.scalar.preload_act_table_set("natural_log_exp_and_others")

            nc.scalar.preload_act_table_set("natural_log_exp_and_others")
            act.wait_ge(ones_set, 2)
            act.wait_ge(const_loaded, 16)
            nc.scalar.activation(sel[:, :], const[0:96, P + 2:P + 2 + 2 * N], ACT.Copy).then_inc(sel_set, 1)
            started = [False]

            def first_step(i, par, s):
                if not started[0]:
                    started[0] = True
                    copy_b(0, 0)
                    copy_b(0, 1)
                step(i, par, s)

            run(act, first_step, dense, lambda: None)

        @block.gpsimd
        def _(pool):
            def step(i, par, s):
                q, n = segment(s)
                g = i * STEPS + s
                if s == 3:
                    add_new(i - 1, 1 - par, 0)
                if s == 3 * N + 3:
                    add_new(i, par, 1)
                if n == 0:
                    wait(pool, u_done, SEGS * i + q + 1)
                wait(pool, b_copied, g + 1)
                wait(pool, scan_done, 2 * (g - 3))
                nc.gpsimd.tensor_tensor(du[:, s % 4, :, :], u[:, q, :, :],
                                        bB[:, s % 4, :].unsqueeze(1).broadcast_to([P, H2, T]),
                                        ALU.mult).then_inc(du_done, 1)

            def add_new(i, par, c):
                if isinstance(i, int) and i < 0:
                    return
                wait(pool, yz_done, 2 * i + 2 - c)
                nc.gpsimd.tensor_tensor(x[par][:, c, :, :], x[par][:, c, :, :], yz[:, :, :],
                                        ALU.add).then_inc(x_new, 1)

            def dense(j, par, t):
                for c in range(2):
                    if t == AT[f"var{c}"] + 4:
                        wait(pool, rstd_done, 2 * j + c + 1)
                        wait(pool, sq_done, 2 * j + c + 1)
                        nc.gpsimd.tensor_tensor(xc[:, :, :], xc[:, :, :],
                                                rstd[:, :].unsqueeze(1).broadcast_to([P, H2, T]),
                                                ALU.mult).then_inc(xn_done, 1)
                for q in range(SEGS):
                    c = CHUNK[q]
                    xd = xs[par][:, q, :, :] if q < 2 else xb[:, q - 2, :, :]
                    if t == AT[f"conv{q}1"] + 5:
                        wait(pool, sp_ready, SOFTPLUSES * j + 2 * q + 1)
                        nc.gpsimd.tensor_tensor(xd, xd, a_conv[:, :, :], ALU.add).then_inc(sp_done, 1)
                    if t == AT[f"dt{q}1"] + 5:
                        wait(pool, sp_ready, SOFTPLUSES * j + 2 * q + 2)
                        nc.gpsimd.tensor_tensor(delta[:, q, :, :], delta[:, q, :, :], a_dt[:, :, :],
                                                ALU.add).then_inc(sp_done, 1)
                        if q >= 2:
                            wait(pool, sp_done, SOFTPLUSES * j + 2 * q + 1)
                            nc.gpsimd.tensor_tensor(xs[par][:, c, :, :], xs[par][:, c, :, :], xd,
                                                    ALU.add).then_inc(xs_done, 1)
                    if t == AT[f"dt{q}1"] + 6:
                        wait(pool, sp_done, SOFTPLUSES * j + 2 * q + 2)
                        wait(pool, du_done, (j - 1) * STEPS + (q + 1) * N)
                        nc.gpsimd.tensor_tensor(u[:, q, :, :], delta[:, q, :, :], xd,
                                                ALU.mult).then_inc(u_done, 1)

            run(pool, step, dense, lambda: add_new(ITEMS - 1, 1, 0))

        @block.vector
        def _(dve):
            def product(i, s):
                if s < 0:
                    i, s = i - 1, s + STEPS
                g = i * STEPS + s
                wait(dve, scan_done, 2 * g + 2)
                wait(dve, c_ready, g + 1)
                wait(dve, sum_done, g - 1)
                dve.tensor_tensor(prod[:, s % 2, :, :], hh[:, s % 4, :, :],
                                  psC[:, s % 2, :].unsqueeze(1).broadcast_to([P, H2, T]),
                                  ALU.mult).then_inc(prod_done, 1)

            def gate(i, par, c):
                done = STEPS if c == 0 else 3 * N
                wait(dve, sum_done, i * STEPS + done)
                wait(dve, z_done, i + 1)
                wait(dve, x_new, 2 * i + 1 - c)
                dve.tensor_tensor(yz[:, :, :], psY[:, :, :], z[par][:, c, :, :], ALU.mult).then_inc(yz_done, 1)

            def step(i, par, s):
                q, n = segment(s)
                g = i * STEPS + s
                first = isinstance(i, int) and i == 0
                way = forward if q < 2 else backward
                wait(dve, du_done, g + 1)
                wait(dve, prod_done, g - 3)
                saved = i * 2 * N + (q // 2) * N + n + 1
                if q % 2:
                    wait(dve, state_saved, saved)
                else:
                    wait(dve, state_saved, saved - 5 if n >= 4 else saved - n - 1)
                for h in range(H2):
                    wait(dve, dA_ready, 2 * g + 1 + h)
                    initial = state[:, n, h:h + 1] if q % 2 else 0.0
                    dve.tensor_tensor_scan(way(hh[:, s % 4, h, :]), way(psA[:, h, :]), way(du[:, s % 4, h, :]),
                                           initial, ALU.mult, ALU.add).then_inc(scan_done, 1)
                if s == 2 and not first:
                    gate(i - 1, 1 - par, 0)
                if s == 3 * N + 2:
                    gate(i, par, 1)
                if not (first and s == 0):
                    product(i, s - 1)

            def dense(j, par, t):
                for c in range(2):
                    if t == AT[f"mean{c}"] + 1:
                        use = j * NU + USE[f"mean{c}"] + 1
                        wait(dve, psd_ready, use)
                        wait(dve, psd_ready, j * NU + USE["proj01"] + 1 if c else (j - 1) * NU + USE["proj11"] + 1)
                        dve.tensor_tensor(xc[:, :, :], x[par][:, c, :, :],
                                          psD[:, :].unsqueeze(1).broadcast_to([P, H2, T]),
                                          ALU.subtract).then_inc(psd_free, 1)
                for q in range(SEGS):
                    if t == AT[f"dbc{q}"] + 1:
                        wait(dve, hi_done, SEGS * j + q + 1)
                        wait(dve, bc_done, SEGS * j + q)
                        dve.scalar_tensor_tensor(out=bc_rest[:, :], in0=bc_hi[:, :], scalar=neg_mask[0],
                                                 in1=psD[0:96, :], op0=ALU.mult, op1=ALU.add
                                                 ).then_inc(psd_free, 1)
                    if t == AT[f"dbc{q}"] + 3:
                        wait(dve, mid_done, SEGS * j + q + 1)
                        wait(dve, c_ready, (j - 1) * STEPS + (q + 1) * N)
                        dve.scalar_tensor_tensor(out=bc[:, q, :], in0=bc_mid[:, :], scalar=neg_mask[1],
                                                 in1=bc_rest[:, :], op0=ALU.mult, op1=ALU.add
                                                 ).then_inc(bc_done, 1)

            def tail():
                product(ITEMS - 1, STEPS - 1)
                gate(ITEMS - 1, 1, 0)

            dve.memset(ones[:, :], 1.0 / C).then_inc(ones_set, 1)
            dve.memset(eps[:, :], 1e-5).then_inc(ones_set, 1)
            dve.wait_ge(const_loaded, 16)
            run(dve, step, dense, tail)


HW = 16
BANDS = 4
PIX = HW * HW
PAIRS = B // 2
BLOCKS = B * PIX // P
KER = 7
PAD = HW + KER - 1
TAPS = 2 * KER * KER
HID = C // 16
OUT_TILES = BANDS * H2
K_TILES = BANDS * H2
V_ONE = 0
V_TWO = V_ONE + 5 * H2
V_CA1 = V_TWO + 5 * OUT_TILES
V_CA2 = V_CA1 + H2 * HID
V_SA = V_CA2 + C
V_COLS = V_SA + TAPS


def wavelet_attention(nc, x_dram, fuse_w, proj_w, vec_in, const_in, pad_dram, gate_dram, out):
    with ExitStack() as ctx:
        def sb(name, shape, dt=F32):
            return ctx.enter_context(nc.sbuf_tensor(name, shape, dt))

        def sem(name):
            return ctx.enter_context(nc.semaphore(name))

        X = mybir.AxisListType.X
        image = sb("image", [P, H2, B, 2 * HW, 2 * HW])
        fw = sb("fw", [P, K_TILES, C])
        pw = sb("pw", [P, H2, OUT_TILES * P])
        vec = sb("vec", [P, V_COLS])
        ident = sb("ident2", [P, P])
        half_sums = sb("half_sums", [P, 4, 2 * PIX])
        bands = sb("bands", [P, 2, BANDS, H2, 2 * PIX])
        fused = sb("fused", [P, H2, B, PIX])
        bn_eps = sb("bn_eps", [P, 1])
        inv = [sb("inv1", [P, H2]), sb("inv2", [P, OUT_TILES])]
        log_v = [sb("log_v1", [P, H2]), sb("log_v2", [P, OUT_TILES])]
        shift = [sb("shift1", [P, H2]), sb("shift2", [P, OUT_TILES])]
        stat = sb("stat", [P, 2, BLOCKS])
        stat_rows = sb("stat_rows", [2 * BLOCKS, P])
        zeros = sb("zeros", [2 * B, PAD * PAD])
        window = sb("window", [P, 2, KER, PAD])
        taps = sb("taps", [P, KER, 2 * KER, HW])
        sp_map = sb("sp_map", [P, HW])
        sp_exp = sb("sp_exp", [P, HW])
        gate = sb("gate", [P, B * PIX])
        pooled = sb("pooled", [P, H2, 2, B])
        hid = sb("hid", [HID, 2, B])
        hid_sum = sb("hid_sum", [HID, B])
        ch_map = sb("ch_map", [P, H2, B])

        banks = [ctx.enter_context(nc.psum_tensor(f"bank{k}", [P, T], F32)) for k in range(6)]
        psP = ctx.enter_context(nc.psum_tensor("psP", [P, 2 * BLOCKS + 3 * P], F32))
        psM = ctx.enter_context(nc.psum_tensor("psM", [P, T], F32))

        image_loaded = [sem(f"image_loaded{k}") for k in range(PAIRS)]
        fw_loaded = sem("fw_loaded")
        pw_loaded = sem("pw_loaded")
        vec_loaded = sem("vec_loaded")
        v_chain = sem("v_chain")
        logs_done = sem("logs_done")
        invs_done = sem("invs_done")
        haar_done = sem("haar_done")
        fuse_ready = sem("fuse_ready")
        fused_done = sem("fused_done")
        turned = sem("turned")
        stats_read = sem("stats_read")
        stat_ready = sem("stat_ready")
        stat_turned = sem("stat_turned")
        rows_done = sem("rows_done")
        border_done = sem("border_done")
        zeros_set = sem("zeros_set")
        pad_stored = sem("pad_stored")
        window_loaded = sem("window_loaded")
        map_ready = sem("map_ready")
        map_exp = sem("map_exp")
        map_done = sem("map_done")
        gate_stored = sem("gate_stored")
        gate_loaded = sem("gate_loaded")
        pooled_done = sem("pooled_done")
        hid_ready = sem("hid_ready")
        hid_relu = sem("hid_relu")
        hid_done = sem("hid_done")
        ca_ready = sem("ca_ready")
        ca_exp = sem("ca_exp")
        scaled_done = sem("scaled_done")
        proj_ready = sem("proj_ready")
        proj_read = sem("proj_read")
        image_done = sem("image_done")
        stored = sem("stored")

        block = ctx.enter_context(nc.Block())

        @block.sync
        def _(sp):
            for k in range(PAIRS):
                for h in range(H2):
                    sp.dma_start(image[:, h, 2 * k:2 * k + 2, :, :].rearrange("p b y x -> p b (y x)"),
                                 x_dram[2 * k:2 * k + 2, h].rearrange("b p c t -> p b (c t)")
                                 ).then_inc(image_loaded[k], 16)
                if k == 0:
                    sp.dma_start(vec[:, :], vec_in).then_inc(vec_loaded, 16)
                    sp.dma_start(ident[:, :], const_in[:, 0:P]).then_inc(vec_loaded, 16)
                    sp.dma_start(fw[:, :, :], fuse_w).then_inc(fw_loaded, 16)
            sp.dma_start(pw[:, :, :], proj_w).then_inc(pw_loaded, 16)
            sp.wait_ge(zeros_set, 2)
            sp.dma_start(pad_dram.rearrange("c b y x -> (c b) (y x)"), zeros[:, :]).then_inc(border_done, 16)
            sp.wait_ge(border_done, 16)
            sp.wait_ge(rows_done, 1)
            lo, hi = KER // 2, KER // 2 + HW
            for c in range(2):
                for b in range(B):
                    r = c * BLOCKS + 2 * b
                    sp.dma_start(pad_dram[c, b, lo:hi, lo:hi].rearrange("(r y) x -> r y x", r=2),
                                 stat_rows[r:r + 2, :].rearrange("r (y x) -> r y x", x=HW)
                                 ).then_inc(pad_stored, 16)
            sp.wait_ge(pad_stored, 16 * 2 * B)
            for c in range(2):
                for dy in range(KER):
                    sp.dma_start(window[:, c, dy, :], pad_dram[c, :, dy:dy + HW, :]
                                 ).then_inc(window_loaded, 16)
            sp.wait_ge(map_done, 1)
            sp.dma_start(gate_dram.rearrange("o (p x) -> (o p) x", p=P), sp_map[:, :]).then_inc(gate_stored, 16)
            sp.wait_ge(gate_stored, 16)
            sp.dma_start(gate[:, :], gate_dram.broadcast_to([P, B * PIX])).then_inc(gate_loaded, 16)
            for k in range(PAIRS):
                for h in range(H2):
                    sp.wait_ge(image_done, k * H2 + h + 1)
                    sp.dma_start(out[2 * k:2 * k + 2, h].rearrange("b p c t -> p b (c t)"),
                                 image[:, h, 2 * k:2 * k + 2, :, :].rearrange("p b y x -> p b (y x)")
                                 ).then_inc(stored, 16)
            sp.wait_ge(stored, 16 * PAIRS * H2)

        @block.tensor
        def _(pe):
            pe.wait_ge(vec_loaded, 32)
            pe.wait_ge(fw_loaded, 16)
            for k in range(PAIRS):
                pe.wait_ge(haar_done, H2 * (k + 1))
                for e in range(H2):
                    u = k * H2 + e
                    if u >= 6:
                        pe.wait_ge(fused_done, u - 5)
                    for t in range(K_TILES):
                        mm = pe.matmul(banks[u % 6][:, :], fw[:, t, e * P:(e + 1) * P],
                                       bands[:, k % 2, t // H2, t % H2, :],
                                       start=(t == 0), stop=(t == K_TILES - 1))
                    mm.then_inc(fuse_ready, 1)
            pe.wait_ge(fused_done, PAIRS * H2)
            for v in range(BLOCKS // 2):
                if v >= 6:
                    pe.wait_ge(stats_read, v - 5)
                for j in range(2):
                    blk = 2 * v + j
                    for h in range(H2):
                        mm = pe.transpose(banks[v % 6][:, (j * H2 + h) * P:(j * H2 + h + 1) * P],
                                          fused[:, h, blk // 2, (blk % 2) * P:(blk % 2 + 1) * P], ident[:, :])
                mm.then_inc(turned, 1)
            pe.wait_ge(stat_ready, 1)
            pe.transpose(psP[0:2 * BLOCKS, 0:P], stat[:, :, :].rearrange("p c k -> p (c k)"),
                         ident[:, :]).then_inc(stat_turned, 1)
            pe.wait_ge(pooled_done, 1)
            for h in range(H2):
                mm = pe.matmul(psM[0:HID, 0:2 * B], vec[:, V_CA1 + h * HID:V_CA1 + (h + 1) * HID],
                               pooled[:, h, :, :].rearrange("p c b -> p (c b)"),
                               start=(h == 0), stop=(h == H2 - 1))
            mm.then_inc(hid_ready, 1)
            pe.wait_ge(hid_done, 1)
            for h in range(H2):
                mm = pe.matmul(psM[:, h * B:(h + 1) * B], vec[0:HID, V_CA2 + h * P:V_CA2 + (h + 1) * P],
                               hid_sum[:, :], start=True, stop=True)
            mm.then_inc(ca_ready, 1)
            pe.wait_ge(pw_loaded, 16)
            for k in range(PAIRS):
                pe.wait_ge(scaled_done, k + 1)
                for o in range(OUT_TILES):
                    u = k * OUT_TILES + o
                    if u >= 6:
                        pe.wait_ge(proj_read, u - 5)
                    for h in range(H2):
                        mm = pe.matmul(banks[u % 6][:, :], pw[:, h, o * P:(o + 1) * P],
                                       fused[:, h, 2 * k:2 * k + 2, :].rearrange("p b x -> p (b x)"),
                                       start=(h == 0), stop=(h == H2 - 1))
                    mm.then_inc(proj_ready, 1)

        @block.scalar
        def _(act):
            act.wait_ge(vec_loaded, 32)
            act.wait_ge(zeros_set, 2)
            for k, (at, m) in enumerate(((V_ONE, H2), (V_TWO, OUT_TILES))):
                nc.scalar.activation(log_v[k][:, :], vec[:, at + 4 * m:at + 5 * m], ACT.Ln,
                                     bias=bn_eps[:, :]).then_inc(logs_done, 1)
            for k in range(2):
                act.wait_ge(logs_done, k + 1)
                nc.scalar.activation(inv[k][:, :], log_v[k][:, :], ACT.Exp, scale=-0.5).then_inc(invs_done, 1)
            act.wait_ge(v_chain, 11)
            for k in range(PAIRS):
                for e in range(H2):
                    act.wait_ge(fuse_ready, k * H2 + e + 1)
                    nc.scalar.activation(fused[:, e, 2 * k:2 * k + 2, :].rearrange("p b x -> p (b x)"),
                                         banks[(k * H2 + e) % 6][:, :], ACT.Relu,
                                         scale=inv[0][:, e:e + 1], bias=shift[0][:, e:e + 1]
                                         ).then_inc(fused_done, 1)
            act.wait_ge(stat_turned, 1)
            nc.scalar.activation(stat_rows[:, :], psP[0:2 * BLOCKS, 0:P], ACT.Copy).then_inc(rows_done, 1)
            act.wait_ge(map_ready, 1)
            nc.scalar.activation(sp_exp[:, :], sp_map[:, :], ACT.Exp, scale=-1.0).then_inc(map_exp, 1)
            act.wait_ge(hid_ready, 1)
            nc.scalar.activation(hid[:, :, :].rearrange("p c b -> p (c b)"), psM[0:HID, 0:2 * B],
                                 ACT.Relu).then_inc(hid_relu, 1)
            act.wait_ge(ca_ready, 1)
            nc.scalar.activation(ch_map[:, :, :].rearrange("p h b -> p (h b)"), psM[:, 0:H2 * B],
                                 ACT.Exp, scale=-1.0).then_inc(ca_exp, 1)
            for k in range(PAIRS):
                if k >= 2:
                    act.wait_ge(image_done, H2 * (k - 1))
                for o in range(OUT_TILES):
                    u = k * OUT_TILES + o
                    act.wait_ge(proj_ready, u + 1)
                    nc.scalar.activation(bands[:, k % 2, o // H2, o % H2, :], banks[u % 6][:, :], ACT.Relu,
                                         scale=inv[1][:, o:o + 1], bias=shift[1][:, o:o + 1]
                                         ).then_inc(proj_read, 1)

        @block.vector
        def _(dve):
            chained = [0]

            def link(ins):
                chained[0] += 1
                ins.then_inc(v_chain, 1)
                dve.wait_ge(v_chain, chained[0])

            dve.memset(bn_eps[:, :], 1e-5).then_inc(zeros_set, 1)
            dve.memset(zeros[:, :], 0.0).then_inc(zeros_set, 1)
            dve.wait_ge(vec_loaded, 32)
            dve.wait_ge(invs_done, 2)
            for k, (at, m) in enumerate(((V_ONE, H2), (V_TWO, OUT_TILES))):
                bias, g, b, mean = (vec[:, at + r * m:at + (r + 1) * m] for r in range(4))
                link(dve.tensor_tensor(inv[k][:, :], inv[k][:, :], g, ALU.mult))
                link(dve.tensor_tensor(shift[k][:, :], bias, mean, ALU.subtract))
                link(dve.tensor_tensor(shift[k][:, :], shift[k][:, :], inv[k][:, :], ALU.mult))
                link(dve.tensor_tensor(shift[k][:, :], shift[k][:, :], b, ALU.add))
            link(dve.tensor_scalar(inv[0][:, :], inv[0][:, :], 0.5, None, ALU.mult))
            link(dve.tensor_scalar(inv[1][:, :], inv[1][:, :], 0.5, None, ALU.mult))
            link(dve.tensor_scalar(shift[1][:, :], shift[1][:, :], 0.5, None, ALU.mult))

            def corners(h, k):
                v = image[:, h, 2 * k:2 * k + 2, :, :].rearrange("p b (y r) (x s) -> p r s (b y) x", r=2, s=2)
                return [v[:, r, s, :, :] for r in range(2) for s in range(2)]

            def flat(ap):
                return ap.rearrange("p (y x) -> p y x", x=HW)

            sums = [flat(half_sums[:, r, :]) for r in range(4)]
            for k in range(PAIRS):
                dve.wait_ge(image_loaded[k], 32)
                if k >= 2:
                    dve.wait_ge(fuse_ready, H2 * (k - 1))
                for h in range(H2):
                    a, b, c, d = corners(h, k)
                    dve.tensor_tensor(sums[0], a, b, ALU.add)
                    dve.tensor_tensor(sums[1], c, d, ALU.add)
                    dve.tensor_tensor(sums[2], a, b, ALU.subtract)
                    link(dve.tensor_tensor(sums[3], c, d, ALU.subtract))
                    for band, (r, op) in enumerate(((0, ALU.add), (0, ALU.subtract),
                                                    (2, ALU.add), (2, ALU.subtract))):
                        ins = dve.tensor_tensor(flat(bands[:, k % 2, band, h, :]), sums[r], sums[r + 1], op)
                    ins.then_inc(haar_done, 1)
                    dve.wait_ge(haar_done, k * H2 + h + 1)
            for v in range(BLOCKS // 2):
                dve.wait_ge(turned, v + 1)
                turn = banks[v % 6][:, :].rearrange("p (j c) -> p j c", j=2)
                dve.tensor_reduce(stat[:, 0, 2 * v:2 * v + 2], turn, X, ALU.add)
                dve.tensor_reduce(stat[:, 1, 2 * v:2 * v + 2], turn, X, ALU.max).then_inc(stats_read, 1)
            dve.wait_ge(stats_read, BLOCKS // 2)
            dve.tensor_scalar(stat[:, 0, :], stat[:, 0, :], 1.0 / C, None, ALU.mult).then_inc(stat_ready, 1)
            dve.wait_ge(window_loaded, 16 * 2 * KER)
            w_sa = vec[:, V_SA:V_SA + TAPS].rearrange("p (d k) -> p k d", k=KER)
            win = window[:, :, :, :].rearrange("p c d x -> p (c d) x")
            for dx in range(KER):
                ins = dve.tensor_tensor(taps[:, dx, :, :], win[:, :, dx:dx + HW],
                                        w_sa[:, dx, :].unsqueeze(2).broadcast_to([P, 2 * KER, HW]), ALU.mult)
            link(ins)
            dve.tensor_reduce(sp_map[:, :], taps[:, :, :, :].rearrange("p k d x -> p x (k d)"), X,
                              ALU.add).then_inc(map_ready, 1)
            dve.wait_ge(map_exp, 1)
            link(dve.tensor_scalar(sp_exp[:, :], sp_exp[:, :], 1.0, None, ALU.add))
            dve.reciprocal(sp_map[:, :], sp_exp[:, :]).then_inc(map_done, 1)
            dve.wait_ge(gate_loaded, 16)
            for h in range(H2):
                rows = fused[:, h, :, :].rearrange("p b x -> p (b x)")
                link(dve.tensor_tensor(rows, rows, gate[:, :], ALU.mult))
            for h in range(H2):
                dve.tensor_reduce(pooled[:, h, 0, :], fused[:, h, :, :], X, ALU.add)
                ins = dve.tensor_reduce(pooled[:, h, 1, :], fused[:, h, :, :], X, ALU.max)
            link(ins)
            dve.tensor_scalar(pooled[:, :, 0, :], pooled[:, :, 0, :], 1.0 / PIX, None, ALU.mult
                              ).then_inc(pooled_done, 1)
            dve.wait_ge(hid_relu, 1)
            dve.tensor_tensor(hid_sum[:, :], hid[:, 0, :], hid[:, 1, :], ALU.add).then_inc(hid_done, 1)
            dve.wait_ge(ca_exp, 1)
            link(dve.tensor_scalar(ch_map[:, :, :], ch_map[:, :, :], 1.0, None, ALU.add))
            link(dve.reciprocal(ch_map[:, :, :], ch_map[:, :, :]))
            for b in range(B):
                for h in range(H2):
                    ins = dve.tensor_scalar(fused[:, h, b, :], fused[:, h, b, :], ch_map[:, h, b:b + 1], None,
                                            ALU.mult)
                if b % 2:
                    ins.then_inc(scaled_done, 1)
            for k in range(PAIRS):
                for h in range(H2):
                    dve.wait_ge(proj_read, k * OUT_TILES + (BANDS - 1) * H2 + h + 1)
                    ll, lh, hl, hh = (flat(bands[:, k % 2, band, h, :]) for band in range(BANDS))
                    dve.tensor_tensor(sums[0], ll, lh, ALU.add)
                    dve.tensor_tensor(sums[1], hl, hh, ALU.add)
                    dve.tensor_tensor(sums[2], ll, lh, ALU.subtract)
                    link(dve.tensor_tensor(sums[3], hl, hh, ALU.subtract))
                    dve.tensor_tensor(ll, sums[0], sums[1], ALU.add)
                    dve.tensor_tensor(lh, sums[0], sums[1], ALU.subtract)
                    dve.tensor_tensor(hl, sums[2], sums[3], ALU.add)
                    link(dve.tensor_tensor(hh, sums[2], sums[3], ALU.subtract))
                    for corner, part in zip(corners(h, k), (ll, lh, hl, hh)):
                        ins = dve.tensor_tensor(corner, corner, part, ALU.add)
                    ins.then_inc(image_done, 1)
                    dve.wait_ge(image_done, k * H2 + h + 1)


def pack_wavelet(inputs):
    import numpy as np

    def arr(name):
        return np.asarray(inputs["L1_conv_" + name])

    def cols(a):
        return a.reshape(-1, P).T

    fuse = arr("fusion_w").T.reshape(K_TILES, P, C).transpose(1, 0, 2)
    proj = arr("proj_w").T.reshape(H2, P, OUT_TILES * P).transpose(1, 0, 2)
    vec = np.zeros((P, V_COLS), np.float32)
    for k, name in enumerate(("fusion_b", "bn1_g", "bn1_b", "bn1_m", "bn1_v")):
        vec[:, V_ONE + k * H2:V_ONE + (k + 1) * H2] = cols(arr(name))
    for k, name in enumerate(("proj_b", "bn2_g", "bn2_b", "bn2_m", "bn2_v")):
        vec[:, V_TWO + k * OUT_TILES:V_TWO + (k + 1) * OUT_TILES] = cols(arr(name))
    w1 = arr("ca_w1").T
    for h in range(H2):
        vec[:, V_CA1 + h * HID:V_CA1 + (h + 1) * HID] = w1[h * P:(h + 1) * P]
    vec[:HID, V_CA2:V_CA2 + C] = arr("ca_w2").T
    vec[:, V_SA:] = arr("sa_w").reshape(1, TAPS)
    return np.ascontiguousarray(fuse), np.ascontiguousarray(proj), vec


def kernel(**inputs):
    import numpy as np
    import concourse.bacc as _bacc
    from concourse.bass_utils import run_bass_kernel_spmd as _run

    def arr(name):
        return np.ascontiguousarray(inputs[name])

    f32 = np.float32
    w = np.zeros((LAYERS, P, W_COLS), f32)

    def put(at, mat):
        m = mat.shape[2]
        for h in range(H2):
            w[:, :, at + h * m:at + (h + 1) * m] = mat[:, h * P:(h + 1) * P]

    put(W_PROJ, arr("L0_conv_proj_w").transpose(0, 2, 1))
    put(W_CONV[0], arr("L0_conv_convf_w").transpose(0, 2, 1))
    put(W_CONV[1], arr("L0_conv_convb_w").transpose(0, 2, 1))
    dbc = arr("L0_conv_dbc_w").transpose(0, 2, 1)
    rows = list(range(R, R + 2 * N))
    put(W_DBC, dbc[:, :, rows * 3 + list(range(R))])
    w[:, 96:, W_DT:W_DT + C] = arr("L0_conv_dtp_w").transpose(0, 2, 1)
    for at, name in ((W_G, "ln_g"), (W_B, "ln_b"), (W_PB, "proj_b"), (W_CB[0], "convf_b"),
                     (W_CB[1], "convb_b"), (W_DTB, "dtp_b"), (W_D, "D_param")):
        w[:, :, at:at + H2] = arr("L0_conv_" + name).reshape(LAYERS, H2, P).transpose(0, 2, 1)
    w[:, :, W_A:] = arr("L0_conv_A_log").reshape(LAYERS, H2, P, N).transpose(0, 2, 1, 3).reshape(LAYERS, P, H2 * N)

    const = np.zeros((P, P + 2 + 2 * N), f32)
    const[:, :P] = np.eye(P)
    const[32:96, P] = -1
    const[64:96, P + 1] = -1
    for k in range(3):
        const[32 * k:32 * (k + 1), P + 2:] = np.eye(32)

    fuse, proj, vec = pack_wavelet(inputs)

    nc = _bacc.Bacc("TRN2", target_bir_lowering=False, num_devices=1)
    arrays = {"x_in": arr("x").reshape(B, H2, P, 2, T), "w_in": w, "const_in": const,
              "fuse_in": fuse, "proj_in": proj, "vec_in": vec}
    aps = {k: nc.dram_tensor(k, v.shape, F32, kind="ExternalInput").ap() for k, v in arrays.items()}
    out = nc.dram_tensor("x_out", (B, H2, P, 2, T), F32, kind="ExternalOutput").ap()
    x_dram = nc.dram_tensor("x_layers", (B, H2, P, 2, T), F32, kind="Internal").ap()
    scan_layers(nc, aps["x_in"], aps["w_in"], aps["const_in"], x_dram)
    pad = nc.dram_tensor("pad_maps", (2, B, PAD, PAD), F32, kind="Internal").ap()
    gate = nc.dram_tensor("gate_row", (1, B * PIX), F32, kind="Internal").ap()
    wavelet_attention(nc, x_dram, aps["fuse_in"], aps["proj_in"], aps["vec_in"], aps["const_in"], pad, gate, out)
    r = _run(nc, [arrays], core_ids=[0])
    return r.results[0]["x_out"].reshape(B, C, 32, 32)
```

```python
from contextlib import ExitStack

import concourse.bass as bass
from concourse import mybir

F32 = mybir.dt.float32
BF16 = mybir.dt.bfloat16
ALU = mybir.AluOpType
ACT = mybir.ActivationFunctionType

P = 128
LAYERS = 12
B = 8
C = 256
H2 = C // P
L = 1024
T = 512
TB = T // P
N = 16
R = 32
ITEMS = LAYERS * B
SEGS = 4
CHUNK = [0, 1, 1, 0]
STEPS = SEGS * N
SOFTPLUSES = 2 * SEGS
B_AHEAD = 3
LAG = 3

W_PROJ = 0
W_CONV = [W_PROJ + H2 * C, W_PROJ + 2 * H2 * C]
W_DBC = W_CONV[1] + H2 * C
W_DT = W_DBC + H2 * P
W_G = W_DT + C
W_B = W_G + H2
W_PB = W_B + H2
W_CB = [W_PB + H2, W_PB + 2 * H2]
W_DTB = W_CB[1] + H2
W_D = W_DTB + H2
W_A = W_D + H2
W_COLS = W_A + H2 * N

USES = [("bias", 17), ("mean0", 19), ("var0", 22), ("proj00", 26), ("proj01", 27),
        ("conv00", 28), ("conv01", 29), ("mean1", 31), ("var1", 34), ("dbc0", 36),
        ("dt00", 38), ("dt01", 39), ("proj10", 40), ("proj11", 41),
        ("conv10", 42), ("conv11", 43), ("dbc1", 50), ("dt10", 52), ("dt11", 53),
        ("conv20", 55), ("conv21", 56), ("dbc2", 63), ("dt20", 65), ("dt21", 66),
        ("conv30", 69), ("conv31", 70), ("dbc3", 77), ("dt30", 79), ("dt31", 80)]
NU = len(USES)
USE = {name: k for k, (name, _) in enumerate(USES)}
AT = dict(USES)
DENSE_END = 90


def scan_layers(nc, x_in, w_all, const_in, x_dram):
    with ExitStack() as ctx:
        def sb(name, shape, dt=F32):
            return ctx.enter_context(nc.sbuf_tensor(name, shape, dt))

        def ps(name, shape):
            return ctx.enter_context(nc.psum_tensor(name, shape, F32))

        def sem(name):
            return ctx.enter_context(nc.semaphore(name))

        const = sb("const", [P, P + 2 + 2 * N])
        ident = const[:, 0:P]
        neg_mask = [const[0:96, P:P + 1], const[0:96, P + 1:P + 2]]
        ones = sb("ones", [P, P])
        eps = sb("eps", [P, 1])
        sel = sb("sel", [96, 2 * N], BF16)
        w = [sb(f"w{p}", [P, W_COLS]) for p in range(2)]
        x = [sb(f"x{p}", [P, 2, H2, T]) for p in range(2)]
        z = sb("z", [P, 2, H2, T])
        xf = [sb(f"xf{p}", [P, 2, H2, T]) for p in range(2)]
        negA = [sb(f"negA{p}", [P, H2, N]) for p in range(2)]
        expA = sb("expA", [P, H2 * N])
        diagD = [sb(f"diagD{p}", [P, H2, P]) for p in range(2)]
        gW = sb("gW", [P, H2, C])
        pbias = sb("pbias", [P, H2])
        delta = sb("delta", [P, SEGS, H2, T])
        u = sb("u", [P, SEGS, H2, T])
        bc = sb("bc", [96, SEGS, T], BF16)
        xc = sb("xc", [P, H2, T])
        sq = sb("sq", [P, H2, T])
        lnv = sb("lnv", [P, T])
        rstd = sb("rstd", [P, T])
        xp = sb("xp", [P, 2, H2, T])
        a_conv = sb("a_conv", [P, H2, T])
        a_dt = sb("a_dt", [P, H2, T])
        xb = sb("xb", [P, 2, H2, T])
        bc_hi = sb("bc_hi", [96, T], BF16)
        bc_mid = sb("bc_mid", [96, T], BF16)
        bc_rest = sb("bc_rest", [96, T])
        dt_low = sb("dt_low", [P, T])
        bB = sb("bB", [P, 4, T])
        du = sb("du", [P, 4, H2, T])
        hh = sb("hh", [P, 4, H2, T])
        state = sb("state", [P, N, H2])
        prod = sb("prod", [P, 4, H2, T])
        y_save = sb("y_save", [P, TB, C])
        y_out = sq[:, :, :].rearrange("p h t -> p (h t)").rearrange("p (k c) -> p k c", c=C)
        yz = sb("yz", [P, H2, T])

        psA = ps("psA", [P, H2, T])
        psC = ps("psC", [P, 2, T])
        psY = ps("psY", [P, H2, T])
        sums = psY[:, :, :].rearrange("p h t -> p (h t)").rearrange("p (k c) -> p k c", c=C)
        psB = ps("psB", [P, T])
        psD = ps("psD", [P, T])

        const_loaded = sem("const_loaded")
        ones_set = sem("ones_set")
        sel_set = sem("sel_set")
        w_loaded = [sem(f"w_loaded{p}") for p in range(2)]
        x_loaded = [sem(f"x_loaded{p}") for p in range(2)]
        x_stored = sem("x_stored")
        psd_ready = sem("psd_ready")
        psd_free = sem("psd_free")
        sq_done = sem("sq_done")
        rstd_done = sem("rstd_done")
        xn_done = sem("xn_done")
        abs_done = sem("abs_done")
        exp_done = sem("exp_done")
        sp_ready = sem("sp_ready")
        sp_done = sem("sp_done")
        hi_done = sem("hi_done")
        mid_done = sem("mid_done")
        bc_done = sem("bc_done")
        u_done = sem("u_done")
        z_done = sem("z_done")
        expA_done = sem("expA_done")
        prep_done = sem("prep_done")
        gw_done = sem("gw_done")
        b_ready = sem("b_ready")
        b_copied = sem("b_copied")
        c_ready = sem("c_ready")
        du_done = sem("du_done")
        dA_ready = sem("dA_ready")
        scan_done = sem("scan_done")
        prod_done = sem("prod_done")
        sum_done = sem("sum_done")
        d_done = sem("d_done")
        state_saved = sem("state_saved")
        y_saved = sem("y_saved")
        y_copied = sem("y_copied")
        y_turned = sem("y_turned")
        yz_done = sem("yz_done")
        x_new = sem("x_new")

        def wait(eng, semaphore, value):
            if not isinstance(value, int) or value > 0:
                eng.wait_ge(semaphore, value)

        def run(eng, step, dense, tail):
            for t in range(STEPS):
                dense(0, 0, t)

            def pair(i0, last=False):
                for par in range(2):
                    i = i0 + par
                    for s in range(STEPS):
                        def others():
                            if STEPS + s < DENSE_END:
                                dense(i, par, STEPS + s)
                            if not (last and par == 1):
                                dense(i + 1, 1 - par, s)

                        step(i, par, s, others)

            pair(0)
            with eng.Fori(2, ITEMS - 2, 2) as i:
                pair(i)
            pair(ITEMS - 2, last=True)
            tail()

        def loads(j, par, each):
            return (j - par) * (each // 2) + each

        def forward(ap):
            return ap

        def backward(ap):
            return ap[:, ::-1]

        def segment(s):
            q, n = divmod(s, N)
            return q, n

        block = ctx.enter_context(nc.Block())

        @block.sync
        def _(sp):
            def load_w(layer, p):
                sp.dma_start(w[p][:, :], w_all[layer]).then_inc(w_loaded[p], 16)

            def load_x(layer, b, i):
                sp.wait_ge(x_stored, 16 * 2 * B + (i - 1) * 32)
                for h in range(H2):
                    sp.dma_start(x[b % 2][:, :, h, :], x_dram[b, h]).then_inc(x_loaded[b % 2], 16)

            def item(i, layer, b):
                more = not (isinstance(i, int) and i >= ITEMS - 2)
                nl, nb = layer + (b + 2) // B, (b + 2) % B
                for k, c in enumerate((1, 0)):
                    sp.wait_ge(x_new, 2 * i + k + 1)
                    sp.dma_start(x_dram[b, :, :, c, :].rearrange("h p t -> p h t"),
                                 x[b % 2][:, c, :, :]).then_inc(x_stored, 16)
                    if more and c == 1:
                        wait(sp, psd_free, (i + 1) * NU)
                        load_w(nl, b % 2)
                if more:
                    load_x(nl, nb, i + 2)

            sp.dma_start(const[:, :], const_in).then_inc(const_loaded, 16)
            for p in range(2):
                load_w(0, p)
                for h in range(H2):
                    sp.dma_start(x[p][:, :, h, :], x_in[p, h]).then_inc(x_loaded[p], 16)
            for b in range(B):
                for h in range(H2):
                    sp.dma_start(x_dram[b, h], x_in[b, h]).then_inc(x_stored, 16)
            sp.wait_ge(x_stored, 16 * 2 * B)
            for b in range(B):
                item(b, 0, b)
            with sp.Fori(1, LAYERS - 1) as layer:
                for b in range(B):
                    item(layer * B + b, layer, b)
            for b in range(B):
                item((LAYERS - 1) * B + b, LAYERS - 1, b)
            sp.wait_ge(x_stored, 16 * 2 * B + ITEMS * 32)

        @block.tensor
        def _(pe):
            def spread(out, row, q):
                return pe.matmul(out, sel[:, row:row + 1].broadcast_to([96, P]), bc[:, q, :],
                                 start=True, stop=True)

            def spread_b(i, s):
                if s >= STEPS:
                    i, s = i + 1, s - STEPS
                q, n = segment(s)
                g = i * STEPS + s
                if n == 0:
                    wait(pe, bc_done, i * SEGS + q + 1)
                wait(pe, b_copied, g)
                spread(psB[:, :], n, q).then_inc(b_ready, 1)

            def turn(out, data, start, stop):
                return pe.matmul(out, data, ident, start=start, stop=stop, is_transpose=True,
                                 skip_group_check=True)

            def turn_back(i, c):
                wait(pe, y_copied, 2 * i + 2 - c)
                parts = [y_out] if c == 1 else [y_out, y_save]
                for k, part in enumerate(parts):
                    for h in range(H2):
                        for b in range(TB):
                            mm = turn(psY[:, h, b * P:(b + 1) * P], part[:, b, h * P:(h + 1) * P],
                                      start=(k == 0 and b == 0), stop=(k == len(parts) - 1))
                mm.then_inc(y_turned, 1)

            def sum_states(i, par, s):
                q, n = segment(s)
                g = i * STEPS + s
                if s == 0:
                    wait(pe, yz_done, 2 * i)
                if s == N:
                    wait(pe, y_saved, i + 1)
                if s == 3 * N:
                    wait(pe, yz_done, 2 * i + 1)
                last = s in (N - 1, 3 * N - 1, STEPS - 1)
                wait(pe, prod_done, g + 1)
                for b in range(TB):
                    for h in range(H2):
                        mm = turn(sums[:, b, h * P:(h + 1) * P], prod[:, s % 4, h, b * P:(b + 1) * P],
                                  start=(s in (0, N, 3 * N) and b % 2 == 0 and h == 0), stop=last)
                mm.then_inc(sum_done, 1)
                for k in range(2):
                    if s in (N + 4 + 4 * k, 3 * N + 4 + 4 * k):
                        c = 1 if s < 3 * N else 0
                        wait(pe, sp_done, SOFTPLUSES * i + (6 if c == 1 else 8))
                        xd = xf[par][:, c, :, :] if k == 0 else xb[:, 1 - c, :, :]
                        for b in range(TB):
                            for h in range(H2):
                                mm = pe.matmul(sums[:, b, h * P:(h + 1) * P], xd[:, h, b * P:(b + 1) * P],
                                               diagD[par][:, h, :], start=False, stop=False,
                                               skip_group_check=True)
                        if k == 1:
                            mm.then_inc(d_done, 1)

            def step(i, par, s, others):
                q, n = segment(s)
                g = i * STEPS + s
                if not (isinstance(i, int) and i == ITEMS - 1 and s + B_AHEAD + 1 >= STEPS):
                    spread_b(i, s + B_AHEAD + 1)
                wait(pe, prod_done, g - 1)
                spread(psC[:, s % 2, :], N + n, q).then_inc(c_ready, 1)
                if s in (LAG, N + LAG, 3 * N + LAG):
                    if s == LAG and not (isinstance(i, int) and i == 0):
                        turn_back(i - 1, 0)
                    if s == 3 * N + LAG:
                        turn_back(i, 1)
                    others()
                    return
                sums_first = s in (LAG - 1, N + LAG - 1, 3 * N + LAG - 1)
                if not sums_first:
                    others()
                if s in (LAG + 1, N + LAG + 1, 3 * N + LAG + 1):
                    sum_states(i, par, s - LAG - 1)
                if s >= LAG:
                    sum_states(i, par, s - LAG)
                elif not (isinstance(i, int) and i == 0):
                    sum_states(i - 1, 1 - par, STEPS + s - LAG)
                if sums_first:
                    others()

            def dense(j, par, t):
                for name, at in USES:
                    if at != t:
                        continue
                    k = USE[name]
                    wait(pe, psd_free, j * NU + k)
                    if name == "bias":
                        wait(pe, w_loaded[par], loads(j, par, 16))
                        for e in range(H2):
                            for h in range(H2):
                                mm = pe.matmul(psD[:, e:e + 1],
                                               w[par][:, W_PROJ + h * C + e * P:W_PROJ + h * C + (e + 1) * P],
                                               w[par][:, W_B + h:W_B + h + 1],
                                               start=(h == 0), stop=(h == H2 - 1))
                    elif name.startswith("mean"):
                        c = int(name[-1])
                        wait(pe, x_loaded[par], loads(j, par, 32))
                        for h in range(H2):
                            mm = pe.matmul(psD[:, :], ones[:, :], x[par][:, c, h, :],
                                           start=(h == 0), stop=(h == H2 - 1))
                    elif name.startswith("var"):
                        c = int(name[-1])
                        wait(pe, sq_done, 2 * j + c + 1)
                        for h in range(H2):
                            mm = pe.matmul(psD[:, :], ones[:, :], sq[:, h, :],
                                           start=(h == 0), stop=(h == H2 - 1))
                    elif name.startswith("proj"):
                        c, e = int(name[-2]), int(name[-1])
                        wait(pe, gw_done, j + 1)
                        wait(pe, xn_done, 2 * j + c + 1)
                        for h in range(H2):
                            mm = pe.matmul(psD[:, :], gW[:, h, e * P:(e + 1) * P], xc[:, h, :],
                                           start=(h == 0), stop=(h == H2 - 1))
                    elif name.startswith("conv"):
                        q, e = int(name[-2]), int(name[-1])
                        c, direction = CHUNK[q], q // 2
                        for h in range(H2):
                            at_w = W_CONV[direction] + h * C + e * P
                            mm = pe.matmul(psD[:, :], w[par][:, at_w:at_w + P], xp[:, c, h, :],
                                           start=(h == 0), stop=(h == H2 - 1))
                    elif name.startswith("dbc"):
                        q = int(name[-1])
                        wait(pe, sp_done, SOFTPLUSES * j + 2 * q + 1)
                        for h in range(H2):
                            src = xf[par][:, q, h, :] if q < 2 else xb[:, q - 2, h, :]
                            at_w = W_DBC + h * P
                            mm = pe.matmul(psD[:, :], w[par][:, at_w:at_w + P], src,
                                           start=(h == 0), stop=(h == H2 - 1))
                    else:
                        q, e = int(name[-2]), int(name[-1])
                        wait(pe, hi_done, SEGS * j + q + 1)
                        mm = pe.matmul(psD[:, :], w[par][96:P, W_DT + e * P:W_DT + (e + 1) * P],
                                       dt_low[96:P, :], start=True, stop=True)
                    mm.then_inc(psd_ready, 1)

            def tail():
                for s in range(STEPS - LAG, STEPS):
                    sum_states(ITEMS - 1, 1, s)
                turn_back(ITEMS - 1, 0)

            pe.wait_ge(const_loaded, 16)
            pe.wait_ge(ones_set, 2)
            pe.wait_ge(sel_set, 1)
            started = [False]

            def first_step(i, par, s, others):
                if not started[0]:
                    started[0] = True
                    for s0 in range(B_AHEAD + 1):
                        spread_b(0, s0)
                step(i, par, s, others)

            run(pe, first_step, dense, tail)

        @block.scalar
        def _(act):
            def copy_b(i, s):
                g = i * STEPS + s
                wait(act, b_ready, g + 1)
                wait(act, du_done, g - 3)
                nc.scalar.activation(bB[:, s % 4, :], psB[:, :], ACT.Copy).then_inc(b_copied, 1)

            def save_state(i, s):
                q, n = segment(s)
                g = i * STEPS + s
                end = T - 1 if q == 0 else 0
                wait(act, scan_done, 2 * g + 2)
                nc.scalar.activation(state[:, n, :], hh[:, s % 4, :, end], ACT.Copy).then_inc(state_saved, 1)

            def step(i, par, s, others):
                q, n = segment(s)
                g = i * STEPS + s
                if n == 0:
                    wait(act, sp_done, SOFTPLUSES * i + 2 * q + 2)
                    wait(act, prep_done, i + 1)
                exp_dA(par, q, n, 0, g)
                if not (isinstance(i, int) and i == ITEMS - 1 and s + B_AHEAD >= STEPS):
                    copy_b(i, s + B_AHEAD)
                if 2 <= s < N + 2 or 2 * N + 2 <= s < 3 * N + 2:
                    save_state(i, s - 2)
                if s == N + LAG:
                    wait(act, sum_done, i * STEPS + N)
                    wait(act, y_turned, 2 * i)
                    nc.scalar.activation(y_save[:, :, :], sums, ACT.Copy).then_inc(y_saved, 1)
                if s == 3 * N + LAG:
                    copy_sums(i, 1)
                if s == LAG and not (isinstance(i, int) and i == 0):
                    copy_sums(i - 1, 0)
                others()
                exp_dA(par, q, n, 1, g)

            def exp_dA(par, q, n, h, g):
                wait(act, scan_done, 2 * g - 1 + h)
                nc.scalar.activation(psA[:, h, :], delta[:, q, h, :], ACT.Exp,
                                     scale=negA[par][:, h, n:n + 1]).then_inc(dA_ready, 1)

            def copy_sums(i, c):
                wait(act, sum_done, i * STEPS + (STEPS if c == 0 else 3 * N))
                wait(act, y_turned, 2 * i + 1 - c)
                nc.scalar.activation(y_out, sums, ACT.Copy).then_inc(y_copied, 1)

            def read_softplus(j, par, name):
                q, e = int(name[-2]), int(name[-1])
                if name.startswith("conv"):
                    bias = w[par][:, W_CB[q // 2] + e:W_CB[q // 2] + e + 1]
                    positive = xf[par][:, q, e, :] if q < 2 else xb[:, q - 2, e, :]
                    size = a_conv[:, e, :]
                    wait(act, sp_done, SOFTPLUSES * j + 2 * q - 1)
                    if q < 2:
                        wait(act, sum_done, (j - 1) * STEPS)
                    else:
                        wait(act, u_done, SEGS * (j - 1) + q + 1)
                        wait(act, d_done, 2 * (j - 1) + q - 1)
                else:
                    bias = w[par][:, W_DTB + e:W_DTB + e + 1]
                    positive = delta[:, q, e, :]
                    size = a_dt[:, e, :]
                    wait(act, sp_done, SOFTPLUSES * j + 2 * q)
                    wait(act, dA_ready, 2 * ((j - 1) * STEPS + (q + 1) * N))
                    wait(act, u_done, SEGS * (j - 1) + q + 1)
                nc.scalar.activation(positive, psD[:, :], ACT.Relu, bias=bias)
                nc.scalar.activation(size, psD[:, :], ACT.Abs, bias=bias).then_inc(psd_free, 1)

            def dense(j, par, t):
                if t == 11:
                    wait(act, w_loaded[par], loads(j, par, 16))
                    wait(act, prep_done, j)
                    nc.scalar.activation(expA[:, :], w[par][:, W_A:W_A + H2 * N], ACT.Exp).then_inc(expA_done, 1)
                if t == 12:
                    wait(act, sum_done, (j - 1) * STEPS)
                    for h in range(H2):
                        nc.scalar.activation(diagD[par][:, h, :], ident, ACT.Copy,
                                             scale=w[par][:, W_D + h:W_D + h + 1])
                    wait(act, expA_done, j + 1)
                    wait(act, dA_ready, 2 * (j - 1) * STEPS)
                    nc.scalar.activation(negA[par][:, :, :], expA[:, :], ACT.Copy, scale=-1.0).then_inc(prep_done, 1)
                if t == 14:
                    wait(act, psd_ready, (j - 1) * NU + USE["proj11"] + 1)
                    for h in range(H2):
                        a = nc.scalar.activation(gW[:, h, :], w[par][:, W_PROJ + h * C:W_PROJ + (h + 1) * C],
                                                 ACT.Copy, scale=w[par][:, W_G + h:W_G + h + 1])
                    a.then_inc(gw_done, 1)
                for name, at in USES:
                    k = USE[name]
                    ready = j * NU + k + 1
                    kind = name.rstrip("0123")
                    if kind == "bias" and t == at + 1:
                        wait(act, psd_ready, ready)
                        wait(act, psd_free, (j - 1) * NU + USE["proj11"] + 1)
                        for e in range(H2):
                            a = nc.scalar.activation(pbias[:, e:e + 1], psD[:, e:e + 1], ACT.Identity,
                                                     bias=w[par][:, W_PB + e:W_PB + e + 1])
                        a.then_inc(psd_free, 1)
                    if kind == "mean" and t == at + 3:
                        c = int(name[-1])
                        wait(act, psd_free, ready)
                        wait(act, psd_ready, j * NU + USE["var0"] + 1 if c else (j - 1) * NU + USE["var1"] + 1)
                        wait(act, y_turned, 2 * (j - 1))
                        nc.scalar.activation(sq[:, :, :], xc[:, :, :], ACT.Square).then_inc(sq_done, 1)
                    if kind == "var" and t == at + 1:
                        c = int(name[-1])
                        wait(act, psd_ready, ready)
                        wait(act, rstd_done, 2 * j + c)
                        nc.scalar.activation(lnv[:, :], psD[:, :], ACT.Ln, bias=eps[:, :]).then_inc(psd_free, 1)
                    if kind == "var" and t == at + 2:
                        c = int(name[-1])
                        wait(act, psd_free, ready)
                        wait(act, xn_done, 2 * j + c)
                        nc.scalar.activation(rstd[:, :], lnv[:, :], ACT.Exp, scale=-0.5).then_inc(rstd_done, 1)
                    if kind == "proj" and t == at + 1:
                        c, e = int(name[-2]), int(name[-1])
                        wait(act, psd_ready, ready)
                        wait(act, psd_ready, (j - 1) * NU + USE["conv31"] + 1)
                        wait(act, z_done, j)
                        wait(act, psd_free, j * NU + USE["bias"] + 1)
                        nc.scalar.activation(xp[:, c, e, :], psD[:, :], ACT.Identity,
                                             bias=pbias[:, e:e + 1]).then_inc(psd_free, 1)
                    if kind in ("conv", "dt") and t == at + 1:
                        wait(act, psd_ready, ready)
                        read_softplus(j, par, name)
                    if kind in ("conv", "dt") and name[-1] == "1" and t in (at + 2, at + 3):
                        q = int(name[-2])
                        count = SOFTPLUSES * j + 2 * q + (kind == "dt")
                        size = a_conv if kind == "conv" else a_dt
                        if t == at + 2:
                            wait(act, psd_free, ready)
                            nc.scalar.activation(size[:, :, :], size[:, :, :], ACT.Exp,
                                                 scale=-1.0).then_inc(exp_done, 1)
                        else:
                            wait(act, exp_done, count + 1)
                            nc.scalar.activation(size[:, :, :], size[:, :, :], ACT.Ln,
                                                 bias=1.0).then_inc(sp_ready, 1)
                    if kind == "dbc" and t == at + 1:
                        q = int(name[-1])
                        wait(act, psd_ready, ready)
                        nc.scalar.activation(bc_hi[:, :], psD[0:96, :], ACT.Copy)
                        nc.scalar.activation(dt_low[96:P, :], psD[96:P, :], ACT.Copy).then_inc(hi_done, 1)
                    if kind == "dbc" and t == at + 3:
                        q = int(name[-1])
                        wait(act, psd_free, ready)
                        wait(act, bc_done, SEGS * j + q)
                        nc.scalar.activation(bc_mid[:, :], bc_rest[:, :], ACT.Copy).then_inc(mid_done, 1)
                if t == STEPS + 10:
                    nc.scalar.preload_act_table_set("silu_and_others")
                    wait(act, psd_free, j * NU + USE["proj11"] + 1)
                    wait(act, yz_done, 2 * j)
                    nc.scalar.activation(z[:, :, :, :], xp[:, :, :, :], ACT.Silu).then_inc(z_done, 1)
                    nc.scalar.preload_act_table_set("natural_log_exp_and_others")

            nc.scalar.preload_act_table_set("natural_log_exp_and_others")
            act.wait_ge(ones_set, 2)
            act.wait_ge(const_loaded, 16)
            nc.scalar.activation(sel[:, :], const[0:96, P + 2:P + 2 + 2 * N], ACT.Copy).then_inc(sel_set, 1)
            started = [False]

            def first_step(i, par, s, others):
                if not started[0]:
                    started[0] = True
                    for s0 in range(B_AHEAD):
                        copy_b(0, s0)
                step(i, par, s, others)

            run(act, first_step, dense, lambda: copy_sums(ITEMS - 1, 0))

        @block.gpsimd
        def _(pool):
            def step(i, par, s, others):
                q, n = segment(s)
                g = i * STEPS + s
                if s == LAG + 7:
                    add_new(i - 1, 1 - par, 0)
                if s == 3 * N + LAG + 7:
                    add_new(i, par, 1)
                if n == 0:
                    wait(pool, u_done, SEGS * i + q + 1)
                wait(pool, b_copied, g + 1)
                wait(pool, scan_done, 2 * (g - 3))
                nc.gpsimd.tensor_tensor(du[:, s % 4, :, :], u[:, q, :, :],
                                        bB[:, s % 4, :].unsqueeze(1).broadcast_to([P, H2, T]),
                                        ALU.mult).then_inc(du_done, 1)
                others()

            def add_new(i, par, c):
                if isinstance(i, int) and i < 0:
                    return
                wait(pool, yz_done, 2 * i + 2 - c)
                nc.gpsimd.tensor_tensor(x[par][:, c, :, :], x[par][:, c, :, :], yz[:, :, :],
                                        ALU.add).then_inc(x_new, 1)

            def dense(j, par, t):
                for c in range(2):
                    if t == AT[f"var{c}"] + 4:
                        wait(pool, rstd_done, 2 * j + c + 1)
                        wait(pool, sq_done, 2 * j + c + 1)
                        nc.gpsimd.tensor_tensor(xc[:, :, :], xc[:, :, :],
                                                rstd[:, :].unsqueeze(1).broadcast_to([P, H2, T]),
                                                ALU.mult).then_inc(xn_done, 1)
                for q in range(SEGS):
                    xd = xf[par][:, q, :, :] if q < 2 else xb[:, q - 2, :, :]
                    if t == AT[f"conv{q}1"] + 6:
                        wait(pool, sp_ready, SOFTPLUSES * j + 2 * q + 1)
                        nc.gpsimd.tensor_tensor(xd, xd, a_conv[:, :, :], ALU.add).then_inc(sp_done, 1)
                    if t == AT[f"dt{q}1"] + 6:
                        wait(pool, sp_ready, SOFTPLUSES * j + 2 * q + 2)
                        nc.gpsimd.tensor_tensor(delta[:, q, :, :], delta[:, q, :, :], a_dt[:, :, :],
                                                ALU.add).then_inc(sp_done, 1)
                    if t == AT[f"dt{q}1"] + 9:
                        wait(pool, sp_done, SOFTPLUSES * j + 2 * q + 2)
                        wait(pool, du_done, (j - 1) * STEPS + (q + 1) * N)
                        nc.gpsimd.tensor_tensor(u[:, q, :, :], delta[:, q, :, :], xd,
                                                ALU.mult).then_inc(u_done, 1)

            run(pool, step, dense, lambda: add_new(ITEMS - 1, 1, 0))

        @block.vector
        def _(dve):
            def product(i, s):
                if s < 0:
                    i, s = i - 1, s + STEPS
                g = i * STEPS + s
                wait(dve, scan_done, 2 * g + 2)
                wait(dve, c_ready, g + 1)
                wait(dve, sum_done, g - 3)
                dve.tensor_tensor(prod[:, s % 4, :, :], hh[:, s % 4, :, :],
                                  psC[:, s % 2, :].unsqueeze(1).broadcast_to([P, H2, T]),
                                  ALU.mult).then_inc(prod_done, 1)

            def gate(i, par, c):
                wait(dve, y_turned, 2 * i + 2 - c)
                wait(dve, z_done, i + 1)
                wait(dve, x_new, 2 * i + 1 - c)
                dve.tensor_tensor(yz[:, :, :], psY[:, :, :], z[:, c, :, :], ALU.mult).then_inc(yz_done, 1)

            def step(i, par, s, others):
                q, n = segment(s)
                g = i * STEPS + s
                first = isinstance(i, int) and i == 0
                way = forward if q < 2 else backward
                wait(dve, du_done, g + 1)
                wait(dve, prod_done, g - 3)
                saved = i * 2 * N + (q // 2) * N + n + 1
                if q % 2:
                    wait(dve, state_saved, saved)
                else:
                    wait(dve, state_saved, saved - 5 if n >= 4 else saved - n - 1)
                def scan(h):
                    wait(dve, dA_ready, 2 * g + 1 + h)
                    initial = state[:, n, h:h + 1] if q % 2 else 0.0
                    dve.tensor_tensor_scan(way(hh[:, s % 4, h, :]), way(psA[:, h, :]), way(du[:, s % 4, h, :]),
                                           initial, ALU.mult, ALU.add).then_inc(scan_done, 1)

                scan(0)
                if s == LAG + 1 and not first:
                    gate(i - 1, 1 - par, 0)
                if s == 3 * N + LAG + 1:
                    gate(i, par, 1)
                if not (first and s == 0):
                    product(i, s - 1)
                scan(1)
                others()

            def dense(j, par, t):
                for c in range(2):
                    if t == AT[f"mean{c}"] + 1:
                        use = j * NU + USE[f"mean{c}"] + 1
                        wait(dve, psd_ready, use)
                        wait(dve, psd_ready, j * NU + USE["proj01"] + 1 if c else (j - 1) * NU + USE["proj11"] + 1)
                        dve.tensor_tensor(xc[:, :, :], x[par][:, c, :, :],
                                          psD[:, :].unsqueeze(1).broadcast_to([P, H2, T]),
                                          ALU.subtract).then_inc(psd_free, 1)
                for q in range(SEGS):
                    if t == AT[f"dbc{q}"] + 1:
                        wait(dve, hi_done, SEGS * j + q + 1)
                        wait(dve, bc_done, SEGS * j + q)
                        dve.scalar_tensor_tensor(out=bc_rest[:, :], in0=bc_hi[:, :], scalar=neg_mask[0],
                                                 in1=psD[0:96, :], op0=ALU.mult, op1=ALU.add
                                                 ).then_inc(psd_free, 1)
                    if t == AT[f"dbc{q}"] + 3:
                        wait(dve, mid_done, SEGS * j + q + 1)
                        wait(dve, c_ready, (j - 1) * STEPS + (q + 1) * N)
                        dve.scalar_tensor_tensor(out=bc[:, q, :], in0=bc_mid[:, :], scalar=neg_mask[1],
                                                 in1=bc_rest[:, :], op0=ALU.mult, op1=ALU.add
                                                 ).then_inc(bc_done, 1)

            def tail():
                product(ITEMS - 1, STEPS - 1)
                gate(ITEMS - 1, 1, 0)

            dve.memset(ones[:, :], 1.0 / C).then_inc(ones_set, 1)
            dve.memset(eps[:, :], 1e-5).then_inc(ones_set, 1)
            dve.wait_ge(const_loaded, 16)
            run(dve, step, dense, tail)


HW = 16
BANDS = 4
PIX = HW * HW
PAIRS = B // 2
BLOCKS = B * PIX // P
KER = 7
PAD = HW + KER - 1
TAPS = 2 * KER * KER
HID = C // 16
OUT_TILES = BANDS * H2
K_TILES = BANDS * H2
V_ONE = 0
V_TWO = V_ONE + 5 * H2
V_CA1 = V_TWO + 5 * OUT_TILES
V_CA2 = V_CA1 + H2 * HID
V_SA = V_CA2 + C
V_COLS = V_SA + TAPS


def wavelet_attention(nc, x_dram, fuse_w, proj_w, vec_in, const_in, pad_dram, gate_dram, out):
    with ExitStack() as ctx:
        def sb(name, shape, dt=F32):
            return ctx.enter_context(nc.sbuf_tensor(name, shape, dt))

        def sem(name):
            return ctx.enter_context(nc.semaphore(name))

        X = mybir.AxisListType.X
        image = sb("image", [P, H2, B, 2 * HW, 2 * HW])
        fw = sb("fw", [P, K_TILES, C])
        pw = sb("pw", [P, H2, OUT_TILES * P])
        vec = sb("vec", [P, V_COLS])
        ident = sb("ident2", [P, P])
        half_sums = sb("half_sums", [P, 4, 2 * PIX])
        bands = sb("bands", [P, 2, BANDS, H2, 2 * PIX])
        fused = sb("fused", [P, H2, B, PIX])
        bn_eps = sb("bn_eps", [P, 1])
        inv = [sb("inv1", [P, H2]), sb("inv2", [P, OUT_TILES])]
        log_v = [sb("log_v1", [P, H2]), sb("log_v2", [P, OUT_TILES])]
        shift = [sb("shift1", [P, H2]), sb("shift2", [P, OUT_TILES])]
        stat = sb("stat", [P, 2, BLOCKS])
        stat_rows = sb("stat_rows", [2 * BLOCKS, P])
        zeros = sb("zeros", [2 * B, PAD * PAD])
        window = sb("window", [P, 2, KER, PAD])
        taps = sb("taps", [P, KER, 2 * KER, HW])
        sp_map = sb("sp_map", [P, HW])
        sp_exp = sb("sp_exp", [P, HW])
        gate = sb("gate", [P, B * PIX])
        pooled = sb("pooled", [P, H2, 2, B])
        hid = sb("hid", [HID, 2, B])
        hid_sum = sb("hid_sum", [HID, B])
        ch_map = sb("ch_map", [P, H2, B])

        banks = [ctx.enter_context(nc.psum_tensor(f"bank{k}", [P, T], F32)) for k in range(6)]
        psP = ctx.enter_context(nc.psum_tensor("psP", [P, 2 * BLOCKS + 3 * P], F32))
        psM = ctx.enter_context(nc.psum_tensor("psM", [P, T], F32))

        image_loaded = [sem(f"image_loaded{k}") for k in range(PAIRS)]
        fw_loaded = sem("fw_loaded")
        pw_loaded = sem("pw_loaded")
        vec_loaded = sem("vec_loaded")
        v_chain = sem("v_chain")
        logs_done = sem("logs_done")
        invs_done = sem("invs_done")
        haar_done = sem("haar_done")
        fuse_ready = sem("fuse_ready")
        fused_done = sem("fused_done")
        turned = sem("turned")
        stats_read = sem("stats_read")
        stat_ready = sem("stat_ready")
        stat_turned = sem("stat_turned")
        rows_done = sem("rows_done")
        border_done = sem("border_done")
        zeros_set = sem("zeros_set")
        pad_stored = sem("pad_stored")
        window_loaded = sem("window_loaded")
        map_ready = sem("map_ready")
        map_exp = sem("map_exp")
        map_done = sem("map_done")
        gate_stored = sem("gate_stored")
        gate_loaded = sem("gate_loaded")
        pooled_done = sem("pooled_done")
        hid_ready = sem("hid_ready")
        hid_relu = sem("hid_relu")
        hid_done = sem("hid_done")
        ca_ready = sem("ca_ready")
        ca_exp = sem("ca_exp")
        scaled_done = sem("scaled_done")
        proj_ready = sem("proj_ready")
        proj_read = sem("proj_read")
        image_done = sem("image_done")
        stored = sem("stored")

        block = ctx.enter_context(nc.Block())

        @block.sync
        def _(sp):
            for k in range(PAIRS):
                for h in range(H2):
                    sp.dma_start(image[:, h, 2 * k:2 * k + 2, :, :].rearrange("p b y x -> p b (y x)"),
                                 x_dram[2 * k:2 * k + 2, h].rearrange("b p c t -> p b (c t)")
                                 ).then_inc(image_loaded[k], 16)
                if k == 0:
                    sp.dma_start(vec[:, :], vec_in).then_inc(vec_loaded, 16)
                    sp.dma_start(ident[:, :], const_in[:, 0:P]).then_inc(vec_loaded, 16)
                    sp.dma_start(fw[:, :, :], fuse_w).then_inc(fw_loaded, 16)
            sp.dma_start(pw[:, :, :], proj_w).then_inc(pw_loaded, 16)
            sp.wait_ge(zeros_set, 2)
            sp.dma_start(pad_dram.rearrange("c b y x -> (c b) (y x)"), zeros[:, :]).then_inc(border_done, 16)
            sp.wait_ge(border_done, 16)
            sp.wait_ge(rows_done, 1)
            lo, hi = KER // 2, KER // 2 + HW
            for c in range(2):
                for b in range(B):
                    r = c * BLOCKS + 2 * b
                    sp.dma_start(pad_dram[c, b, lo:hi, lo:hi].rearrange("(r y) x -> r y x", r=2),
                                 stat_rows[r:r + 2, :].rearrange("r (y x) -> r y x", x=HW)
                                 ).then_inc(pad_stored, 16)
            sp.wait_ge(pad_stored, 16 * 2 * B)
            for c in range(2):
                for dy in range(KER):
                    sp.dma_start(window[:, c, dy, :], pad_dram[c, :, dy:dy + HW, :]
                                 ).then_inc(window_loaded, 16)
            sp.wait_ge(map_done, 1)
            sp.dma_start(gate_dram.rearrange("o (p x) -> (o p) x", p=P), sp_map[:, :]).then_inc(gate_stored, 16)
            sp.wait_ge(gate_stored, 16)
            sp.dma_start(gate[:, :], gate_dram.broadcast_to([P, B * PIX])).then_inc(gate_loaded, 16)
            for k in range(PAIRS):
                for h in range(H2):
                    sp.wait_ge(image_done, k * H2 + h + 1)
                    sp.dma_start(out[2 * k:2 * k + 2, h].rearrange("b p c t -> p b (c t)"),
                                 image[:, h, 2 * k:2 * k + 2, :, :].rearrange("p b y x -> p b (y x)")
                                 ).then_inc(stored, 16)
            sp.wait_ge(stored, 16 * PAIRS * H2)

        @block.tensor
        def _(pe):
            pe.wait_ge(vec_loaded, 32)
            pe.wait_ge(fw_loaded, 16)
            for k in range(PAIRS):
                pe.wait_ge(haar_done, H2 * (k + 1))
                for e in range(H2):
                    u = k * H2 + e
                    if u >= 6:
                        pe.wait_ge(fused_done, u - 5)
                    for t in range(K_TILES):
                        mm = pe.matmul(banks[u % 6][:, :], fw[:, t, e * P:(e + 1) * P],
                                       bands[:, k % 2, t // H2, t % H2, :],
                                       start=(t == 0), stop=(t == K_TILES - 1))
                    mm.then_inc(fuse_ready, 1)
            pe.wait_ge(fused_done, PAIRS * H2)
            for v in range(BLOCKS // 2):
                if v >= 6:
                    pe.wait_ge(stats_read, v - 5)
                for j in range(2):
                    blk = 2 * v + j
                    for h in range(H2):
                        mm = pe.transpose(banks[v % 6][:, (j * H2 + h) * P:(j * H2 + h + 1) * P],
                                          fused[:, h, blk // 2, (blk % 2) * P:(blk % 2 + 1) * P], ident[:, :])
                mm.then_inc(turned, 1)
            pe.wait_ge(stat_ready, 1)
            pe.transpose(psP[0:2 * BLOCKS, 0:P], stat[:, :, :].rearrange("p c k -> p (c k)"),
                         ident[:, :]).then_inc(stat_turned, 1)
            pe.wait_ge(pooled_done, 1)
            for h in range(H2):
                mm = pe.matmul(psM[0:HID, 0:2 * B], vec[:, V_CA1 + h * HID:V_CA1 + (h + 1) * HID],
                               pooled[:, h, :, :].rearrange("p c b -> p (c b)"),
                               start=(h == 0), stop=(h == H2 - 1))
            mm.then_inc(hid_ready, 1)
            pe.wait_ge(hid_done, 1)
            for h in range(H2):
                mm = pe.matmul(psM[:, h * B:(h + 1) * B], vec[0:HID, V_CA2 + h * P:V_CA2 + (h + 1) * P],
                               hid_sum[:, :], start=True, stop=True)
            mm.then_inc(ca_ready, 1)
            pe.wait_ge(pw_loaded, 16)
            for k in range(PAIRS):
                pe.wait_ge(scaled_done, k + 1)
                for o in range(OUT_TILES):
                    u = k * OUT_TILES + o
                    if u >= 6:
                        pe.wait_ge(proj_read, u - 5)
                    for h in range(H2):
                        mm = pe.matmul(banks[u % 6][:, :], pw[:, h, o * P:(o + 1) * P],
                                       fused[:, h, 2 * k:2 * k + 2, :].rearrange("p b x -> p (b x)"),
                                       start=(h == 0), stop=(h == H2 - 1))
                    mm.then_inc(proj_ready, 1)

        @block.scalar
        def _(act):
            act.wait_ge(vec_loaded, 32)
            act.wait_ge(zeros_set, 2)
            for k, (at, m) in enumerate(((V_ONE, H2), (V_TWO, OUT_TILES))):
                nc.scalar.activation(log_v[k][:, :], vec[:, at + 4 * m:at + 5 * m], ACT.Ln,
                                     bias=bn_eps[:, :]).then_inc(logs_done, 1)
            for k in range(2):
                act.wait_ge(logs_done, k + 1)
                nc.scalar.activation(inv[k][:, :], log_v[k][:, :], ACT.Exp, scale=-0.5).then_inc(invs_done, 1)
            act.wait_ge(v_chain, 11)
            for k in range(PAIRS):
                for e in range(H2):
                    act.wait_ge(fuse_ready, k * H2 + e + 1)
                    nc.scalar.activation(fused[:, e, 2 * k:2 * k + 2, :].rearrange("p b x -> p (b x)"),
                                         banks[(k * H2 + e) % 6][:, :], ACT.Relu,
                                         scale=inv[0][:, e:e + 1], bias=shift[0][:, e:e + 1]
                                         ).then_inc(fused_done, 1)
            act.wait_ge(stat_turned, 1)
            nc.scalar.activation(stat_rows[:, :], psP[0:2 * BLOCKS, 0:P], ACT.Copy).then_inc(rows_done, 1)
            act.wait_ge(map_ready, 1)
            nc.scalar.activation(sp_exp[:, :], sp_map[:, :], ACT.Exp, scale=-1.0).then_inc(map_exp, 1)
            act.wait_ge(hid_ready, 1)
            nc.scalar.activation(hid[:, :, :].rearrange("p c b -> p (c b)"), psM[0:HID, 0:2 * B],
                                 ACT.Relu).then_inc(hid_relu, 1)
            act.wait_ge(ca_ready, 1)
            nc.scalar.activation(ch_map[:, :, :].rearrange("p h b -> p (h b)"), psM[:, 0:H2 * B],
                                 ACT.Exp, scale=-1.0).then_inc(ca_exp, 1)
            for k in range(PAIRS):
                if k >= 2:
                    act.wait_ge(image_done, H2 * (k - 1))
                for o in range(OUT_TILES):
                    u = k * OUT_TILES + o
                    act.wait_ge(proj_ready, u + 1)
                    nc.scalar.activation(bands[:, k % 2, o // H2, o % H2, :], banks[u % 6][:, :], ACT.Relu,
                                         scale=inv[1][:, o:o + 1], bias=shift[1][:, o:o + 1]
                                         ).then_inc(proj_read, 1)

        @block.vector
        def _(dve):
            chained = [0]

            def link(ins):
                chained[0] += 1
                ins.then_inc(v_chain, 1)
                dve.wait_ge(v_chain, chained[0])

            dve.memset(bn_eps[:, :], 1e-5).then_inc(zeros_set, 1)
            dve.memset(zeros[:, :], 0.0).then_inc(zeros_set, 1)
            dve.wait_ge(vec_loaded, 32)
            dve.wait_ge(invs_done, 2)
            for k, (at, m) in enumerate(((V_ONE, H2), (V_TWO, OUT_TILES))):
                bias, g, b, mean = (vec[:, at + r * m:at + (r + 1) * m] for r in range(4))
                link(dve.tensor_tensor(inv[k][:, :], inv[k][:, :], g, ALU.mult))
                link(dve.tensor_tensor(shift[k][:, :], bias, mean, ALU.subtract))
                link(dve.tensor_tensor(shift[k][:, :], shift[k][:, :], inv[k][:, :], ALU.mult))
                link(dve.tensor_tensor(shift[k][:, :], shift[k][:, :], b, ALU.add))
            link(dve.tensor_scalar(inv[0][:, :], inv[0][:, :], 0.5, None, ALU.mult))
            link(dve.tensor_scalar(inv[1][:, :], inv[1][:, :], 0.5, None, ALU.mult))
            link(dve.tensor_scalar(shift[1][:, :], shift[1][:, :], 0.5, None, ALU.mult))

            def corners(h, k):
                v = image[:, h, 2 * k:2 * k + 2, :, :].rearrange("p b (y r) (x s) -> p r s (b y) x", r=2, s=2)
                return [v[:, r, s, :, :] for r in range(2) for s in range(2)]

            def flat(ap):
                return ap.rearrange("p (y x) -> p y x", x=HW)

            sums = [flat(half_sums[:, r, :]) for r in range(4)]
            for k in range(PAIRS):
                dve.wait_ge(image_loaded[k], 32)
                if k >= 2:
                    dve.wait_ge(fuse_ready, H2 * (k - 1))
                for h in range(H2):
                    a, b, c, d = corners(h, k)
                    dve.tensor_tensor(sums[0], a, b, ALU.add)
                    dve.tensor_tensor(sums[1], c, d, ALU.add)
                    dve.tensor_tensor(sums[2], a, b, ALU.subtract)
                    link(dve.tensor_tensor(sums[3], c, d, ALU.subtract))
                    for band, (r, op) in enumerate(((0, ALU.add), (0, ALU.subtract),
                                                    (2, ALU.add), (2, ALU.subtract))):
                        ins = dve.tensor_tensor(flat(bands[:, k % 2, band, h, :]), sums[r], sums[r + 1], op)
                    ins.then_inc(haar_done, 1)
                    dve.wait_ge(haar_done, k * H2 + h + 1)
            for v in range(BLOCKS // 2):
                dve.wait_ge(turned, v + 1)
                turn = banks[v % 6][:, :].rearrange("p (j c) -> p j c", j=2)
                dve.tensor_reduce(stat[:, 0, 2 * v:2 * v + 2], turn, X, ALU.add)
                dve.tensor_reduce(stat[:, 1, 2 * v:2 * v + 2], turn, X, ALU.max).then_inc(stats_read, 1)
            dve.wait_ge(stats_read, BLOCKS // 2)
            dve.tensor_scalar(stat[:, 0, :], stat[:, 0, :], 1.0 / C, None, ALU.mult).then_inc(stat_ready, 1)
            dve.wait_ge(window_loaded, 16 * 2 * KER)
            w_sa = vec[:, V_SA:V_SA + TAPS].rearrange("p (d k) -> p k d", k=KER)
            win = window[:, :, :, :].rearrange("p c d x -> p (c d) x")
            for dx in range(KER):
                ins = dve.tensor_tensor(taps[:, dx, :, :], win[:, :, dx:dx + HW],
                                        w_sa[:, dx, :].unsqueeze(2).broadcast_to([P, 2 * KER, HW]), ALU.mult)
            link(ins)
            dve.tensor_reduce(sp_map[:, :], taps[:, :, :, :].rearrange("p k d x -> p x (k d)"), X,
                              ALU.add).then_inc(map_ready, 1)
            dve.wait_ge(map_exp, 1)
            link(dve.tensor_scalar(sp_exp[:, :], sp_exp[:, :], 1.0, None, ALU.add))
            dve.reciprocal(sp_map[:, :], sp_exp[:, :]).then_inc(map_done, 1)
            dve.wait_ge(gate_loaded, 16)
            for h in range(H2):
                rows = fused[:, h, :, :].rearrange("p b x -> p (b x)")
                link(dve.tensor_tensor(rows, rows, gate[:, :], ALU.mult))
            for h in range(H2):
                dve.tensor_reduce(pooled[:, h, 0, :], fused[:, h, :, :], X, ALU.add)
                ins = dve.tensor_reduce(pooled[:, h, 1, :], fused[:, h, :, :], X, ALU.max)
            link(ins)
            dve.tensor_scalar(pooled[:, :, 0, :], pooled[:, :, 0, :], 1.0 / PIX, None, ALU.mult
                              ).then_inc(pooled_done, 1)
            dve.wait_ge(hid_relu, 1)
            dve.tensor_tensor(hid_sum[:, :], hid[:, 0, :], hid[:, 1, :], ALU.add).then_inc(hid_done, 1)
            dve.wait_ge(ca_exp, 1)
            link(dve.tensor_scalar(ch_map[:, :, :], ch_map[:, :, :], 1.0, None, ALU.add))
            link(dve.reciprocal(ch_map[:, :, :], ch_map[:, :, :]))
            for b in range(B):
                for h in range(H2):
                    ins = dve.tensor_scalar(fused[:, h, b, :], fused[:, h, b, :], ch_map[:, h, b:b + 1], None,
                                            ALU.mult)
                if b % 2:
                    ins.then_inc(scaled_done, 1)
            for k in range(PAIRS):
                for h in range(H2):
                    dve.wait_ge(proj_read, k * OUT_TILES + (BANDS - 1) * H2 + h + 1)
                    ll, lh, hl, hh = (flat(bands[:, k % 2, band, h, :]) for band in range(BANDS))
                    dve.tensor_tensor(sums[0], ll, lh, ALU.add)
                    dve.tensor_tensor(sums[1], hl, hh, ALU.add)
                    dve.tensor_tensor(sums[2], ll, lh, ALU.subtract)
                    link(dve.tensor_tensor(sums[3], hl, hh, ALU.subtract))
                    dve.tensor_tensor(ll, sums[0], sums[1], ALU.add)
                    dve.tensor_tensor(lh, sums[0], sums[1], ALU.subtract)
                    dve.tensor_tensor(hl, sums[2], sums[3], ALU.add)
                    link(dve.tensor_tensor(hh, sums[2], sums[3], ALU.subtract))
                    for corner, part in zip(corners(h, k), (ll, lh, hl, hh)):
                        ins = dve.tensor_tensor(corner, corner, part, ALU.add)
                    ins.then_inc(image_done, 1)
                    dve.wait_ge(image_done, k * H2 + h + 1)


def pack_wavelet(inputs):
    import numpy as np

    def arr(name):
        return np.asarray(inputs["L1_conv_" + name])

    def cols(a):
        return a.reshape(-1, P).T

    fuse = arr("fusion_w").T.reshape(K_TILES, P, C).transpose(1, 0, 2)
    proj = arr("proj_w").T.reshape(H2, P, OUT_TILES * P).transpose(1, 0, 2)
    vec = np.zeros((P, V_COLS), np.float32)
    for k, name in enumerate(("fusion_b", "bn1_g", "bn1_b", "bn1_m", "bn1_v")):
        vec[:, V_ONE + k * H2:V_ONE + (k + 1) * H2] = cols(arr(name))
    for k, name in enumerate(("proj_b", "bn2_g", "bn2_b", "bn2_m", "bn2_v")):
        vec[:, V_TWO + k * OUT_TILES:V_TWO + (k + 1) * OUT_TILES] = cols(arr(name))
    w1 = arr("ca_w1").T
    for h in range(H2):
        vec[:, V_CA1 + h * HID:V_CA1 + (h + 1) * HID] = w1[h * P:(h + 1) * P]
    vec[:HID, V_CA2:V_CA2 + C] = arr("ca_w2").T
    vec[:, V_SA:] = arr("sa_w").reshape(1, TAPS)
    return np.ascontiguousarray(fuse), np.ascontiguousarray(proj), vec


def kernel(**inputs):
    import numpy as np
    import concourse.bacc as _bacc
    from concourse.bass_utils import run_bass_kernel_spmd as _run

    def arr(name):
        return np.ascontiguousarray(inputs[name])

    f32 = np.float32
    w = np.zeros((LAYERS, P, W_COLS), f32)

    def put(at, mat):
        m = mat.shape[2]
        for h in range(H2):
            w[:, :, at + h * m:at + (h + 1) * m] = mat[:, h * P:(h + 1) * P]

    put(W_PROJ, arr("L0_conv_proj_w").transpose(0, 2, 1))
    put(W_CONV[0], arr("L0_conv_convf_w").transpose(0, 2, 1))
    put(W_CONV[1], arr("L0_conv_convb_w").transpose(0, 2, 1))
    dbc = arr("L0_conv_dbc_w").transpose(0, 2, 1)
    rows = list(range(R, R + 2 * N))
    put(W_DBC, dbc[:, :, rows * 3 + list(range(R))])
    w[:, 96:, W_DT:W_DT + C] = arr("L0_conv_dtp_w").transpose(0, 2, 1)
    for at, name in ((W_G, "ln_g"), (W_B, "ln_b"), (W_PB, "proj_b"), (W_CB[0], "convf_b"),
                     (W_CB[1], "convb_b"), (W_DTB, "dtp_b"), (W_D, "D_param")):
        w[:, :, at:at + H2] = arr("L0_conv_" + name).reshape(LAYERS, H2, P).transpose(0, 2, 1)
    w[:, :, W_A:] = arr("L0_conv_A_log").reshape(LAYERS, H2, P, N).transpose(0, 2, 1, 3).reshape(LAYERS, P, H2 * N)

    const = np.zeros((P, P + 2 + 2 * N), f32)
    const[:, :P] = np.eye(P)
    const[32:96, P] = -1
    const[64:96, P + 1] = -1
    for k in range(3):
        const[32 * k:32 * (k + 1), P + 2:] = np.eye(32)

    fuse, proj, vec = pack_wavelet(inputs)

    nc = _bacc.Bacc("TRN2", target_bir_lowering=False, num_devices=1)
    arrays = {"x_in": arr("x").reshape(B, H2, P, 2, T), "w_in": w, "const_in": const,
              "fuse_in": fuse, "proj_in": proj, "vec_in": vec}
    aps = {k: nc.dram_tensor(k, v.shape, F32, kind="ExternalInput").ap() for k, v in arrays.items()}
    out = nc.dram_tensor("x_out", (B, H2, P, 2, T), F32, kind="ExternalOutput").ap()
    x_dram = nc.dram_tensor("x_layers", (B, H2, P, 2, T), F32, kind="Internal").ap()
    scan_layers(nc, aps["x_in"], aps["w_in"], aps["const_in"], x_dram)
    pad = nc.dram_tensor("pad_maps", (2, B, PAD, PAD), F32, kind="Internal").ap()
    gate = nc.dram_tensor("gate_row", (1, B * PIX), F32, kind="Internal").ap()
    wavelet_attention(nc, x_dram, aps["fuse_in"], aps["proj_in"], aps["vec_in"], aps["const_in"], pad, gate, out)
    r = _run(nc, [arrays], core_ids=[0])
    return r.results[0]["x_out"].reshape(B, C, 32, 32)
```
